# Optimizing a Trainium2 kernel written in Bass

```python
import numpy as np
import jax
import jax.numpy as jnp

def _softmax(x, axis=-1):
    return jax.nn.softmax(x, axis=axis)

def _gelu(x):
    return jax.nn.gelu(x, approximate=True)

def _silu(x):
    return jax.nn.silu(x)

def _sigmoid(x):
    return jax.nn.sigmoid(x)

def _layernorm(x, axis=-1, eps=1e-05):
    m = jnp.mean(x, axis=axis, keepdims=True)
    v = jnp.var(x, axis=axis, keepdims=True)
    return (x - m) / jnp.sqrt(v + eps)

def _scatter_add(tgt, idx, src, axis=0):
    return tgt.at[idx].add(src)

def _segment_sum(src, seg, n):
    return jax.ops.segment_sum(src, seg, n)
kernel_name = 'mk_macaron_d1_jaxref_r8_8325b7'

def setup_inputs(seed: int=0):
    np.random.seed(seed)
    _w = jnp.asarray

    def _L0_attn_setup():
        import jax, jax.numpy as jnp
        import numpy as np
        B_SZ, L_SEQ, D_MODEL, D_STATE = (4, 256, 128, 16)

        def _ssm_scan(u, A_log, B_param, C_param, log_dt):
            L = u.shape[1]
            dt = jnp.clip(jnp.exp(log_dt), 0.0001, 1.0)
            A_bar = jnp.exp(-jnp.exp(A_log) * dt[:, None])
            A_bar = jnp.clip(A_bar, 1e-08, 1.0 - 1e-08)
            log_A = jnp.log(A_bar)
            t_idx = jnp.arange(L, dtype=jnp.float32)
            A_powers = jnp.exp(t_idx[:, None, None] * log_A[None, :, :])
            cb_dt = C_param * B_param * dt[:, None]
            kernel = jnp.einsum('ldn,dn->ld', A_powers, cb_dt)
            n_fft = 2 * L
            Kf = jnp.fft.rfft(kernel, n=n_fft, axis=0)
            Uf = jnp.fft.rfft(u, n=n_fft, axis=1)
            y = jnp.fft.irfft(Uf * Kf[None], n=n_fft, axis=1)[:, :L]
            return y.astype(u.dtype)
        key = jax.random.key(seed)
        ks = jax.random.split(key, 6)
        x = jax.random.normal(ks[0], (B_SZ, L_SEQ, D_MODEL), jnp.float32)
        A_log = jnp.clip(jnp.log(jnp.arange(1, D_STATE + 1, dtype=jnp.float32)), -7.0, None)
        A_log = jnp.broadcast_to(A_log[None, :], (D_MODEL, D_STATE)).astype(jnp.float32)
        B_param = 0.02 * jax.random.normal(ks[1], (D_MODEL, D_STATE), jnp.float32)
        C_param = 0.02 * jax.random.normal(ks[2], (D_MODEL, D_STATE), jnp.float32)
        log_dt = 0.01 * jax.random.normal(ks[3], (D_MODEL,), jnp.float32) - 4.0
        in_w = jax.random.normal(ks[4], (2 * D_MODEL, D_MODEL), jnp.float32) / np.sqrt(D_MODEL).astype(np.float32)
        in_b = jnp.zeros((2 * D_MODEL,), jnp.float32)
        out_w = jax.random.normal(ks[5], (D_MODEL, D_MODEL), jnp.float32) / np.sqrt(D_MODEL).astype(np.float32)
        out_b = jnp.zeros((D_MODEL,), jnp.float32)
        ln_g = jnp.ones((D_MODEL,), jnp.float32)
        ln_b = jnp.zeros((D_MODEL,), jnp.float32)
        return {'x': x, 'A_log': A_log, 'B_param': B_param, 'C_param': C_param, 'log_dt': log_dt, 'in_w': in_w, 'in_b': in_b, 'out_w': out_w, 'out_b': out_b, 'ln_g': ln_g, 'ln_b': ln_b}
    _L0_attn_in = _L0_attn_setup()

    def _L0_ffn_setup():
        import jax, jax.numpy as jnp
        import numpy as np
        EPS = 1e-12

        def rms_norm(t, gamma):
            n = jnp.maximum(jnp.linalg.norm(t, axis=-1, keepdims=True), EPS)
            scale = jnp.sqrt(jnp.asarray(t.shape[-1], t.dtype))
            return t / n * scale * gamma
        key = jax.random.key(seed)
        ks = jax.random.split(key, 4)
        b, s, d = (4, 512, 128)
        e, t = (8, 64)
        hidden = 4 * d
        return {'x': jax.random.normal(ks[0], (b, s, d), dtype=jnp.float32), 'gamma_x': jnp.ones((d,), dtype=jnp.float32), 'gamma_slot': jnp.ones((d,), dtype=jnp.float32), 'slot_embeds': jax.random.normal(ks[1], (e, t, d), dtype=jnp.float32), 'w1': jax.random.normal(ks[2], (d, hidden), dtype=jnp.float32) * (1.0 / np.sqrt(d)), 'w2': jax.random.normal(ks[3], (hidden, d), dtype=jnp.float32) * (1.0 / np.sqrt(hidden))}
    _L0_ffn_in = _L0_ffn_setup()
    _d = {'L0_attn_x': _L0_attn_in['x'], 'L0_attn_A_log': _L0_attn_in['A_log'], 'L0_attn_B_param': _L0_attn_in['B_param'], 'L0_attn_C_param': _L0_attn_in['C_param'], 'L0_attn_log_dt': _L0_attn_in['log_dt'], 'L0_attn_in_w': _L0_attn_in['in_w'], 'L0_attn_in_b': _L0_attn_in['in_b'], 'L0_attn_out_w': _L0_attn_in['out_w'], 'L0_attn_out_b': _L0_attn_in['out_b'], 'L0_attn_ln_g': _L0_attn_in['ln_g'], 'L0_attn_ln_b': _L0_attn_in['ln_b'], 'L0_ffn_gamma_x': _L0_ffn_in['gamma_x'], 'L0_ffn_gamma_slot': _L0_ffn_in['gamma_slot'], 'L0_ffn_slot_embeds': _L0_ffn_in['slot_embeds'], 'L0_ffn_w1': _L0_ffn_in['w1'], 'L0_ffn_w2': _L0_ffn_in['w2']}
    _x0 = _d['L0_attn_x']
    _d['L0_attn_x'] = jax.random.normal(jax.random.fold_in(jax.random.key(seed), 1), (32, 256, 128), dtype=_x0.dtype)
    del _x0
    return _d

def reference(L0_attn_x, L0_attn_A_log, L0_attn_B_param, L0_attn_C_param, L0_attn_log_dt, L0_attn_in_w, L0_attn_in_b, L0_attn_out_w, L0_attn_out_b, L0_attn_ln_g, L0_attn_ln_b, L0_ffn_gamma_x, L0_ffn_gamma_slot, L0_ffn_slot_embeds, L0_ffn_w1, L0_ffn_w2):

    def _L0_attn_ref(x, A_log, B_param, C_param, log_dt, in_w, in_b, out_w, out_b, ln_g, ln_b):
        import jax, jax.numpy as jnp
        import numpy as np
        B_SZ, L_SEQ, D_MODEL, D_STATE = (4, 256, 128, 16)

        def _ssm_scan(u, A_log, B_param, C_param, log_dt):
            L = u.shape[1]
            dt = jnp.clip(jnp.exp(log_dt), 0.0001, 1.0)
            A_bar = jnp.exp(-jnp.exp(A_log) * dt[:, None])
            A_bar = jnp.clip(A_bar, 1e-08, 1.0 - 1e-08)
            log_A = jnp.log(A_bar)
            t_idx = jnp.arange(L, dtype=jnp.float32)
            A_powers = jnp.exp(t_idx[:, None, None] * log_A[None, :, :])
            cb_dt = C_param * B_param * dt[:, None]
            kernel = jnp.einsum('ldn,dn->ld', A_powers, cb_dt)
            n_fft = 2 * L
            Kf = jnp.fft.rfft(kernel, n=n_fft, axis=0)
            Uf = jnp.fft.rfft(u, n=n_fft, axis=1)
            y = jnp.fft.irfft(Uf * Kf[None], n=n_fft, axis=1)[:, :L]
            return y.astype(u.dtype)
        x = x.astype(jnp.float32)
        residual = x
        mu = jnp.mean(x, axis=-1, keepdims=True)
        var = jnp.mean(jnp.square(x - mu), axis=-1, keepdims=True)
        xn = (x - mu) * jax.lax.rsqrt(var + 1e-05) * ln_g + ln_b
        xz = xn @ in_w.T + in_b
        x_proj, z = (xz[..., :D_MODEL], xz[..., D_MODEL:])
        z = jax.nn.silu(z)
        y = _ssm_scan(x_proj, A_log, B_param, C_param, log_dt)
        y = y * z
        y = y @ out_w.T + out_b
        return jnp.clip(y + residual, -10.0, 10.0)

    def _L0_ffn_ref(x, gamma_x, gamma_slot, slot_embeds, w1, w2):
        import jax, jax.numpy as jnp
        import numpy as np
        EPS = 1e-12

        def rms_norm(t, gamma):
            n = jnp.maximum(jnp.linalg.norm(t, axis=-1, keepdims=True), EPS)
            scale = jnp.sqrt(jnp.asarray(t.shape[-1], t.dtype))
            return t / n * scale * gamma
        b, s, d = x.shape
        e, t, _ = slot_embeds.shape
        xn = rms_norm(x, gamma_x)
        se = rms_norm(slot_embeds, gamma_slot)
        logits = jnp.einsum('bsd,etd->bset', xn, se)
        dispatch = jax.nn.softmax(logits, axis=1)
        slots = jnp.einsum('bsd,bset->betd', xn, dispatch)
        h = jax.nn.gelu(slots @ w1, approximate=False)
        processed = h @ w2
        combine = jax.nn.softmax(logits.reshape(b, s, e * t), axis=-1)
        out = jnp.einsum('bnd,bsn->bsd', processed.reshape(b, e * t, d), combine)
        return out
    x = L0_attn_x
    x = x + 0.5 * _L0_ffn_ref(_layernorm(x, axis=-1), L0_ffn_gamma_x, L0_ffn_gamma_slot, L0_ffn_slot_embeds, L0_ffn_w1, L0_ffn_w2)
    x = x + _L0_attn_ref(_layernorm(x, axis=-1), L0_attn_A_log, L0_attn_B_param, L0_attn_C_param, L0_attn_log_dt, L0_attn_in_w, L0_attn_in_b, L0_attn_out_w, L0_attn_out_b, L0_attn_ln_g, L0_attn_ln_b)
    x = x + 0.5 * _L0_ffn_ref(_layernorm(x, axis=-1), L0_ffn_gamma_x, L0_ffn_gamma_slot, L0_ffn_slot_embeds, L0_ffn_w1, L0_ffn_w2)
    return x

_drawn_inputs = setup_inputs


def setup_inputs(seed=0):
    import zlib

    import numpy as np

    out = dict(_drawn_inputs(seed))
    spreads = {'L0_attn_in_b': (0.0, 2.0),
     'L0_attn_out_b': (0.0, 0.1),
     'L0_attn_ln_g': (1.0, 0.6),
     'L0_attn_ln_b': (0.0, 0.8),
     'L0_ffn_gamma_x': (1.0, 0.2),
     'L0_ffn_gamma_slot': (1.0, 0.2)}
    factors = {'L0_attn_A_log': 8.0,
     'L0_attn_B_param': 8.0,
     'L0_attn_C_param': 8.0,
     'L0_attn_log_dt': 8.0,
     'L0_attn_in_w': 8.0,
     'L0_attn_out_w': 8.0}
    for name, (base, spread) in spreads.items():
        noise = np.random.default_rng([zlib.crc32(name.encode()), seed]).standard_normal(out[name].shape)
        drawn = base * np.exp(spread * noise) if base else spread * noise
        out[name] = jnp.asarray(drawn.astype(out[name].dtype))
    for name, factor in factors.items():
        out[name] = (out[name] * factor).astype(out[name].dtype)
    return out
```

```python
import math
from contextlib import ExitStack

import concourse.bass as bass
from concourse import mybir

F32 = mybir.dt.float32
F32R = mybir.dt.float32r
F16 = mybir.dt.float16
BF16 = mybir.dt.bfloat16
ALU = mybir.AluOpType
ACT = mybir.ActivationFunctionType
AX = mybir.AxisListType.X

P = 128
LN_EPS = 1e-5
RMS_EPS = 1e-12
LOG_A_MIN = math.log(1e-8)
DT_MIN, DT_MAX = 1e-4, 1.0
CLIP = 10.0
HALF = 4096.0


def macaron_kernel(nc, x_in, A_log, B_param, C_param, log_dt, in_w, in_b, out_w, out_b,
                   ln_g, ln_b, gamma_x, gamma_slot, slot_embeds, w1, w2, out):
    NB, SEQ, D = x_in.shape
    TT = SEQ // P
    NT = NB * TT
    NS = A_log.shape[1]
    SLOTS = slot_embeds.shape[0] * slot_embeds.shape[1]
    ST = SLOTS // P
    HID = w1.shape[1]
    HT = HID // P
    assert D == P and TT == 2 and ST == 4 and HT == 4 and NB % 2 == 0

    CH = 8
    NCH = D // CH
    RING = 6
    LAG0 = SEQ // 2 - 1
    KP = 384
    XCH = 8
    XB = NB // XCH

    x_dram = x_in.rearrange("b (h p) d -> p (b h) d", p=P)
    out_dram = out.rearrange("b (h p) d -> p (b h) d", p=P)
    resp_dram = nc.dram_tensor("resp_dram", [D, 2, KP], F16, kind="Internal")

    ctx = ExitStack()
    with ctx:
        def sb(name, shape, dt=F32, where=ctx):
            return where.enter_context(nc.sbuf_tensor(name, shape, dt))

        def psum(name, shape):
            return ctx.enter_context(nc.psum_tensor(name, shape, F32))

        def sem(name):
            return ctx.enter_context(nc.semaphore(name))

        x = sb("x", [P, NT, D])
        ident = sb("ident", [P, P])
        identb = sb("identb", [P, P], BF16)
        flip = sb("flip", [P, P])
        w1h = sb("w1h", [P, HID], F32R)
        w1l = sb("w1l", [P, HID], F32R)
        w2s = sb("w2s", [P, HT, D])
        seh = sb("seh", [P, SLOTS], F32R)
        sel = sb("sel", [P, SLOTS], F32R)
        inT = sb("inT", [P, 2 * D])
        binh = sb("binh", [P, 2 * D], F32R)
        oneh = sb("oneh", [P, P], F32R)
        outT = sb("outT", [P, D])
        obias = sb("obias", [P, D])
        respp = sb("respp", [P, 2, KP], F16)
        mean_var = sb("mean_var", [P, 2, TT, 2])
        floor_var = sb("floor_var", [P, 2, TT])
        scale_x = sb("scale_x", [P, 2, TT])
        new_mv = sb("new_mv", [P, TT, 2])
        mix_var = sb("mix_var", [P, 2, 2, TT])
        mix_scale = sb("mix_scale", [P, 2, TT])
        mone = sb("mone", [P, 1])
        res2 = sb("res2", [P, TT, D])
        nmean = sb("nmean", [P, NT])
        rstd = sb("rstd", [P, NT])
        mhalf = sb("mhalf", [P, ST])
        bn6 = sb("bn6", [P, 2, 6])
        bnm = sb("bnm", [P, 2, 6])
        u = sb("u", [P, D, 2, 2 * NB], F16)
        z = sb("z", [P, 2, NB, D])
        xm = sb("xm", [P, TT, D])
        xc = sb("xc", [P, TT, D])
        mT = sb("mT", [P, 2 * SEQ])
        upd = sb("upd", [P, TT, D])
        sig = sb("sig", [P, TT, D])
        rsig = sb("rsig", [P, TT, D])

        xn = sb("xn", [P, 2, TT, D + 1], F32)
        xTh = sb("xTh", [P, 2, SEQ], F32R)
        xTl = sb("xTl", [P, 2, SEQ], F32R)
        E_c = sb("E_c", [P, TT, SLOTS], F32)
        E_d = sb("E_d", [P, TT, SLOTS], F32)
        E_cT = sb("E_cT", [P, 2, ST, SEQ], F32)
        slots_n = sb("slots_n", [P, ST, D], F32)
        sTh = sb("sTh", [P, SLOTS], F32R)
        sTl = sb("sTl", [P, SLOTS], F32R)
        hT = sb("hT", [P, HT, SLOTS], F32)
        proc = sb("proc", [P, ST, D], F32)
        colmax = sb("colmax", [P, ST], F32)
        ncolmax = sb("ncolmax", [P, ST], BF16)
        rowmax = sb("rowmax", [P, TT], F32)
        nrowmax = sb("nrowmax", [P, TT], F32)
        rowsum = sb("rowsum", [P, 2, TT], F32)
        rrow = sb("rrow", [P, TT], F32)
        hrrow = sb("hrrow", [P, 2, TT], F32)
        rslot = sb("rslot", [P, 2, 2], F32)
        setup = ExitStack()
        raw_w1 = sb("raw_w1", [P, HID], F32, setup)
        raw_se = sb("raw_se", [P, ST, D], F32, setup)
        raw_in = sb("raw_in", [P, 2, D], F32, setup)
        raw_out = sb("raw_out", [P, D], F32, setup)
        gslot = sb("gslot", [P, D], F32, setup)
        gxrow = sb("gxrow", [P, D], F32, setup)
        grow = sb("grow", [P, D], F32, setup)
        brow = sb("brow", [P, D], F32, setup)
        gxcol = sb("gxcol", [P, 1], F32, setup)
        inb = sb("inb", [P, 2], F32, setup)
        Alog = sb("Alog", [P, NS], F32, setup)
        Bp = sb("Bp", [P, NS], F32, setup)
        Cp = sb("Cp", [P, NS], F32, setup)
        ldt = sb("ldt", [P, 1], F32, setup)
        sq = sb("sq", [P, ST, D], F32, setup)
        ss = sb("ss", [P, ST], F32, setup)
        ms = sb("ms", [P, ST], F32, setup)
        sef = sb("sef", [P, ST], F32, setup)
        se_n = sb("se_n", [P, ST, D], F32, setup)
        w1g = sb("w1g", [P, HID], F32, setup)
        lags = sb("lags", [P, SEQ], F32, setup)
        half = sb("half", [P, NS], F32, setup)
        powers = sb("powers", [P, NS, SEQ], F32, setup)
        resp = sb("resp", [P, SEQ], F32, setup)
        expA = sb("expA", [P, NS], F32, setup)
        expdt = sb("expdt", [P, 1], F32, setup)
        dt = sb("dt", [P, 1], F32, setup)
        logA = sb("logA", [P, NS], F32, setup)
        cb = sb("cb", [P, NS], F32, setup)
        cbn = sb("cbn", [P, NS], F32, setup)
        cbs = sb("cbs", [P, 1], F32, setup)
        rcbs = sb("rcbs", [P, 1], F32, setup)
        inw = sb("inw", [P, 2, D], F32, setup)
        insq = sb("insq", [P, 2, D], F32, setup)
        bias = sb("bias", [P, 2], F32, setup)
        n2 = sb("n2", [P, 1], F32, setup)
        nrm = sb("nrm", [P, 1], F32, setup)
        ubound = sb("ubound", [P, 1], F32, setup)
        rub = sb("rub", [P, 1], F32, setup)
        nbias = sb("nbias", [P, 1], F32, setup)
        oscale = sb("oscale", [P, 1], F32, setup)
        brep = sb("brep", [P, 2 * D], F32, setup)
        setup.close()
        toep = sb("toep", [P, RING, CH, 2, SEQ], F16)
        res, resb, yg, updc = xc, xm, mT[:, SEQ:].rearrange("p (h d) -> p h d", h=TT), sig

        bankL = psum("bankL", [P, TT, SLOTS])
        bankT = psum("bankT", [P, 2, 512])
        bankH = psum("bankH", [P, 2, 512])
        bankM = psum("bankM", [P, 2, 512])
        LT = bankT[:, :, :].rearrange("p a (s t) -> p (a s) t", t=SEQ)
        SC = 130
        slot_ps = bankH[:, :, 0:2 * SC].rearrange("p a (s c) -> p a s c", c=SC)

        w_se, w_w1, w_w2, w_ssm, w_io = (sem(n) for n in ("w_se", "w_w1", "w_w2", "w_ssm", "w_io"))
        x_in_s = [sem(f"x_in{c}") for c in range(XCH)]
        consts = sem("consts")
        dve_seq = sem("dve_seq")
        pool_seq = sem("pool_seq")
        se_sum, se_floor, se_scale, se_row = (sem(n) for n in ("se_sum", "se_floor", "se_scale", "se_row"))
        seT_ps, se_s, w1h_s, w1_s = (sem(n) for n in ("seT_ps", "se_s", "w1h_s", "w1_s"))
        n2_s, nrm_s, in_row, inT_ps, mix_set = (sem(n) for n in ("n2_s", "nrm_s", "in_row", "inT_ps", "mix_set"))
        ssm_exp, logA_s, powers_s, cbs_s = (sem(n) for n in ("ssm_exp", "logA_s", "powers_s", "cbs_s"))
        resp_s = sem("resp_s")
        resp_out = sem("resp_out")
        toep_s = [sem(f"toep{c}") for c in range(RING)]

        bn_s, mv_s, var_s, scale_s = (sem(n) for n in ("bn_s", "mv_s", "var_s", "scale_s"))
        mbn_s, mag_s, mvar_s = (sem(n) for n in ("mbn_s", "mag_s", "mvar_s"))
        xn_s, xT_ps, xTh_s, xT_s = (sem(n) for n in ("xn_s", "xT_ps", "xTh_s", "xT_s"))
        LT_ps, L_ps, Ld_ps = (sem(n) for n in ("LT_ps", "L_ps", "Ld_ps"))
        cmax_s, ncmax_s, rmax_s, nrmax_s = (sem(n) for n in ("cmax_s", "ncmax_s", "rmax_s", "nrmax_s"))
        Ec_s, Ed_s, EcT_ps, EcT_s = (sem(n) for n in ("Ec_s", "Ed_s", "EcT_ps", "EcT_s"))
        rrow_s, hrrow_s = sem("rrow_s"), sem("hrrow_s")
        slots_ps, rslot_s, slots_s = (sem(n) for n in ("slots_ps", "rslot_s", "slots_s"))
        sT_ps, sTh_s, sT_s = (sem(n) for n in ("sT_ps", "sTh_s", "sT_s"))
        h_ps, gelu_s, proc_ps, proc_s = (sem(n) for n in ("h_ps", "gelu_s", "proc_ps", "proc_s"))
        out_ps, x_s = sem("out_ps"), sem("x_s")

        mscale_s, xc_s, xm_s, mT_ps, mT_s = (sem(n) for n in ("mscale_s", "xc_s", "xm_s", "mT_ps", "mT_s"))
        uz_ps, e_s, zc_s, uh_s, u_s = (sem(n) for n in ("uz_ps", "e_s", "zc_s", "uh_s", "u_s"))
        e1_s, sig_s, z_s = (sem(n) for n in ("e1_s", "sig_s", "z_s"))
        conv_ps, y_s = sem("conv_ps"), sem("y_s")
        yg_s, ygT_ps, ygT_s, o_ps = (sem(n) for n in ("yg_s", "ygT_ps", "ygT_s", "o_ps"))
        rc_s, res_s, resb_s, upd_s, updc_s, mixed = (sem(n) for n in ("rc_s", "res_s", "resb_s", "upd_s", "updc_s", "mixed"))
        stored = sem("stored")

        block = ctx.enter_context(nc.Block())

        def steps(eng, body, first, loop_from, loop_to, last):
            for i in range(first, loop_from):
                body(i, i % 2, lambda k, i=i: 0 <= i + k < NB)
            with eng.Fori(0, (loop_to - loop_from) // 2, 1) as j:
                for p in range(2):
                    body(j * 2 + (loop_from + p), (loop_from + p) % 2, lambda k: True)
            for i in range(loop_to, last + 1):
                body(i, i % 2, lambda k, i=i: 0 <= i + k < NB)

        def h_bank(k):
            return (bankH[:, 0, :], bankH[:, 1, :], bankM[:, 0, :], bankH[:, 0, :])[k]

        def i_is(i, n):
            return type(i) is int and i == n

        def tile(t, n=1):
            return x[:, bass.ds(t, n), :]

        FFN1 = dict(first=-3, loop_from=3, loop_to=NB - 3, last=NB + 2)
        FFN2 = dict(first=-4, loop_from=2, loop_to=NB - 4, last=NB - 1)
        CONV_ROUNDS = NCH // RING

        def split3(eng, out_ap, ah, al, bh, bl, stop=True, start=True):
            eng.matmul(out_ap, ah, bh, start=start, stop=False)
            eng.matmul(out_ap, ah, bl, start=False, stop=False)
            return eng.matmul(out_ap, al, bh, start=False, stop=stop)

        def toeplitz(s, c, part, lag):
            return toep[:, s, c, part, lag:lag + P]

        def u_part(part, b):
            v = u[:, :, part, :].rearrange("p c (h b) -> p h c b", h=2)
            return v[:, :, :, bass.ds(b, 1)].rearrange("p h c o -> p h (c o)")

        u32 = u[:, :, :, :].rearrange("p c s n -> p (c s n)").bitcast(F32).rearrange("p (c n) -> p c n", n=2 * NB)

        def y_of(c, n):
            return u32[:, bass.ds(c, n), :]

        def conv_bank(s):
            b = (bankH, bankM, bankL)[s // 2]
            return b[:, s % 2, :].rearrange("p (c n) -> p c n", n=2 * NB)

        def conv_rounds(eng, chunk):
            with eng.Fori(0, CONV_ROUNDS, 1) as j:
                for s in range(RING):
                    chunk(j * RING + s, s, j)
            for s in range(NCH - CONV_ROUNDS * RING):
                chunk(CONV_ROUNDS * RING + s, s, CONV_ROUNDS)

        @block.sync
        def _(sp):
            sp.dma_start(raw_se[:, :, :], slot_embeds.rearrange("e t d -> (e t) d")
                         .rearrange("(s p) d -> p s d", p=P)).then_inc(w_se, 16)
            for c in range(XCH):
                sp.dma_start(x[:, c * XB * TT:(c + 1) * XB * TT, :],
                             x_dram[:, c * XB * TT:(c + 1) * XB * TT, :]).then_inc(x_in_s[c], 16)
                if c == 0:
                    sp.dma_start(raw_w1[:, :], w1).then_inc(w_w1, 16)
                    sp.dma_start(w2s[:, :, :], w2.rearrange("(k p) d -> p k d", p=P)).then_inc(w_w2, 16)
            sp.wait_ge(resp_s, 4)
            sp.dma_start(resp_dram[:, :, :], respp[:, :, :]).then_inc(resp_out, 16)
            sp.wait_ge(resp_out, 16)
            sp.wait_ge(mix_set, 1)
            for c in range(NCH):
                s = c % RING
                if c >= RING:
                    sp.wait_ge(conv_ps, c - RING + 1)
                for part in range(2):
                    src = bass.AP(resp_dram, c * CH * 2 * KP + part * KP,
                                  [[1, P], [2 * KP, CH], [1, SEQ]])
                    sp.dma_start(toep[:, s, :, part, :], src).then_inc(toep_s[s], 16)
            with sp.Fori(0, NB // 2, 1) as j:
                sp.wait_ge(x_s, j * 2 + (NB + 2))
                sp.dma_start(out_dram[:, bass.ds(j * 4, 4), :], x[:, bass.ds(j * 4, 4), :]).then_inc(stored, 16)
            sp.wait_ge(stored, 16 * (NB // 2))

        @block.gpsimd
        def _(pool):
            pool.memset(ident[:, :], 0.0).then_inc(consts, 1)
            pool.memset(identb[:, :], 0.0).then_inc(consts, 1)
            pool.memset(flip[:, :], 0.0).then_inc(consts, 1)
            pool.wait_ge(consts, 3)
            for m in (ident, identb):
                pool.affine_select(out=m[:, :], in_=m[:, :], compare_op=ALU.not_equal, fill=1.0, base=0,
                                   pattern=[[-1, P]], channel_multiplier=1).then_inc(consts, 1)
            pool.affine_select(out=flip[:, :], in_=flip[:, :], compare_op=ALU.not_equal, fill=1.0, base=1 - P,
                               pattern=[[1, P]], channel_multiplier=1).then_inc(consts, 1)
            pool.iota(lags[:, :], pattern=[[1, SEQ]], base=0, channel_multiplier=0,
                      allow_small_or_imprecise_dtypes=True).then_inc(consts, 1)
            pool.memset(mhalf[:, :], -0.5).then_inc(consts, 1)
            pool.memset(half[:, :], 0.5).then_inc(consts, 1)
            pool.memset(mone[:, :], -1.0).then_inc(consts, 1)
            pool.wait_ge(consts, 10)
            count = [0]

            def link(ins):
                count[0] += 1
                ins.then_inc(pool_seq, 1)
                pool.wait_ge(pool_seq, count[0])

            pool.wait_ge(se_floor, 1)
            pool.tensor_tensor(sef[:, :], ms[:, :], mhalf[:, :], ALU.pow).then_inc(se_scale, 1)
            pool.wait_ge(ssm_exp, 2)
            link(pool.tensor_scalar(dt[:, :], expdt[:, :], DT_MIN, DT_MAX, ALU.max, ALU.min))
            link(pool.tensor_scalar(logA[:, :], expA[:, :], dt[:, 0:1], -1.0, ALU.mult, ALU.mult))
            pool.tensor_scalar(logA[:, :], logA[:, :], LOG_A_MIN, 0.0, ALU.max, ALU.min).then_inc(logA_s, 1)

            def gains():
                link(pool.tensor_tensor(cb[:, :], Bp[:, :], Cp[:, :], ALU.mult))
                link(pool.tensor_scalar(cb[:, :], cb[:, :], dt[:, 0:1], None, ALU.mult))
                link(pool.tensor_tensor(cbn[:, :], cb[:, :], cb[:, :], ALU.mult))
                link(pool.tensor_tensor(cbn[:, :], cbn[:, :], half[:, :], ALU.pow))
                n = NS // 2
                while n:
                    link(pool.tensor_tensor(cbn[:, 0:n], cbn[:, 0:n], cbn[:, n:2 * n], ALU.add))
                    n //= 2
                link(pool.tensor_scalar(cbs[:, :], cbn[:, 0:1], 1e-18, 1.01 / HALF, ALU.max, ALU.mult))
                link(pool.tensor_tensor(rcbs[:, :], cbs[:, :], mone[:, :], ALU.pow))
                pool.tensor_scalar(cb[:, :], cb[:, :], rcbs[:, 0:1], None, ALU.mult).then_inc(cbs_s, 1)
                pool.wait_ge(cbs_s, 1)

            def response(q):
                n = NS // 2
                pool.wait_ge(powers_s, (q + 1) * n)
                mine = powers[:, q * n:(q + 1) * n, :]
                link(pool.tensor_tensor(mine, mine, cb[:, q * n:(q + 1) * n].unsqueeze(2).to_broadcast([P, n, SEQ]),
                                        ALU.mult))
                while n > 1:
                    n //= 2
                    link(pool.tensor_tensor(mine[:, 0:n, :], mine[:, 0:n, :], mine[:, n:2 * n, :], ALU.add))
                if q == 1:
                    link(pool.tensor_tensor(resp[:, :], powers[:, 0, :], powers[:, NS // 2, :], ALU.add))

            def response_parts():
                pool.memset(respp[:, :, 0:LAG0], 0.0).then_inc(resp_s, 1)
                pool.memset(respp[:, :, LAG0 + SEQ:KP], 0.0).then_inc(resp_s, 1)
                pool.tensor_copy(respp[:, 0, LAG0:LAG0 + SEQ], resp[:, :]).then_inc(resp_s, 1)
                pool.wait_ge(resp_s, 3)
                pool.tensor_tensor(respp[:, 1, LAG0:LAG0 + SEQ], resp[:, :], respp[:, 0, LAG0:LAG0 + SEQ],
                                   ALU.subtract).then_inc(resp_s, 1)

            def centred(dst, b, done, value):
                t = b * TT
                pool.tensor_tensor(dst, tile(t, TT), nmean[:, bass.ds(t, TT)].unsqueeze(2).to_broadcast([P, TT, D]),
                                   ALU.add).then_inc(done, 1)
                pool.wait_ge(done, value)

            def ffn_scale(base, i, par, has):
                if has(3):
                    pool.wait_ge(var_s, i + (base + 4))
                    pool.tensor_tensor(scale_x[:, 1 - par, :], floor_var[:, 1 - par, :], mhalf[:, 0:TT], ALU.pow)\
                        .then_inc(scale_s, 1)

            def body1(i, par, has):
                if has(-2):
                    pool.wait_ge(mscale_s, i - 1)
                    if has(-3):
                        pool.wait_ge(mT_ps, i - 2)
                    centred(xc[:, :, :], i - 2, xc_s, i - 1)
                    pool.tensor_tensor(xm[:, :, :], xc[:, :, :], mix_scale[:, par, :].unsqueeze(2).to_broadcast([P, TT, D]),
                                       ALU.mult).then_inc(xm_s, 1)
                ffn_scale(0, i, par, has)
                if has(-1):
                    pool.wait_ge(mvar_s, 2 * i)
                    pool.tensor_tensor(rstd[:, bass.ds((i - 1) * TT, TT)], mix_var[:, 1, 1 - par, :], mhalf[:, 0:TT],
                                       ALU.pow)
                    pool.tensor_tensor(mix_scale[:, 1 - par, :], mix_var[:, 0, 1 - par, :], mhalf[:, 0:TT],
                                       ALU.pow).then_inc(mscale_s, 1)
                if i_is(i, -2):
                    gains()
                if i_is(i, -1):
                    pool.wait_ge(n2_s, 1)
                    pool.tensor_tensor(nrm[:, :], n2[:, :], mhalf[:, 0:1], ALU.pow).then_inc(nrm_s, 1)
                for q in range(2):
                    if i_is(i, q):
                        response(q)
                if i_is(i, 2):
                    response_parts()

            def body2(i, par, has):
                if has(4):
                    c = i + 4
                    if has(3):
                        pool.wait_ge(upd_s, c)
                    centred(res[:, :, :], c, rc_s, i + 5)
                    pool.tensor_tensor(res2[:, :, :], res[:, :, :],
                                       rstd[:, bass.ds(c * TT, TT)].unsqueeze(2).to_broadcast([P, TT, D]),
                                       ALU.mult).then_inc(res_s, 1)
                    pool.wait_ge(res_s, i + 5)
                    pool.tensor_tensor(resb[:, :, :], res2[:, :, :], obias[:, :].unsqueeze(1).to_broadcast([P, TT, D]),
                                       ALU.add).then_inc(resb_s, 1)
                ffn_scale(NB, i, par, has)

            steps(pool, body1, **FFN1)
            pool.wait_ge(mT_ps, NB)
            pool.wait_ge(mscale_s, NB)
            steps(pool, body2, **FFN2)

        @block.scalar
        def _(act):
            act.dma_start(gslot[:, :], gamma_slot.partition_broadcast(P)).then_inc(w_se, 16)
            act.dma_start(gxrow[:, :], gamma_x.partition_broadcast(P)).then_inc(w_se, 16)
            act.dma_start(gxcol[:, :], gamma_x.rearrange("(d o) -> d o", o=1)).then_inc(w_w1, 16)
            for dst, src in ((Alog, A_log), (Bp, B_param), (Cp, C_param)):
                act.dma_start(dst[:, :], src).then_inc(w_ssm, 16)
            act.dma_start(ldt[:, :], log_dt.rearrange("(d o) -> d o", o=1)).then_inc(w_ssm, 16)
            act.dma_start(raw_in[:, :, :], in_w.rearrange("(r p) d -> p r d", p=P)).then_inc(w_io, 16)
            for r in range(2):
                act.dma_start(inb[:, r:r + 1], in_b[r * P:(r + 1) * P].rearrange("(p o) -> p o", o=1)).then_inc(w_io, 16)
            act.dma_start(raw_out[:, :], out_w).then_inc(w_io, 16)
            act.dma_start(obias[:, :], out_b.partition_broadcast(P)).then_inc(w_io, 16)
            act.dma_start(grow[:, :], ln_g.partition_broadcast(P)).then_inc(w_io, 16)
            act.dma_start(brow[:, :], ln_b.partition_broadcast(P)).then_inc(w_io, 16)
            act.wait_ge(w_se, 48)
            for s in range(ST):
                e = act.activation(sq[:, s, :], raw_se[:, s, :], ACT.Square, accum_out=ss[:, s:s + 1])
            e.then_inc(se_sum, 1)
            act.wait_ge(w_ssm, 64)
            act.activation(expA[:, :], Alog[:, :], ACT.Exp).then_inc(ssm_exp, 1)
            act.activation(expdt[:, :], ldt[:, :], ACT.Exp).then_inc(ssm_exp, 1)
            act.wait_ge(w_w1, 32)
            act.activation(w1h[:, :], raw_w1[:, :], ACT.Copy, scale=gxcol[:, 0:1]).then_inc(w1h_s, 1)
            act.wait_ge(logA_s, 1)
            act.wait_ge(consts, 7)
            for n in range(NS):
                act.activation(powers[:, n, :], lags[:, :], ACT.Exp, scale=logA[:, n:n + 1]).then_inc(powers_s, 1)

            def second_half(base, i):
                act.wait_ge(sT_ps, i + (base + 1))
                act.activation(sTh[:, :], bankM[:, 0, :], ACT.Copy).then_inc(sTh_s, 1)
                for k in range(HT):
                    act.wait_ge(h_ps, i * HT + (base * HT + k + 1))
                    act.activation(hT[:, k, :], h_bank(k), ACT.Gelu).then_inc(gelu_s, 1)

            def combine_weights(base, i, nxt):
                act.wait_ge(nrmax_s, i + (base + 2))
                for t in range(TT):
                    act.activation(E_c[:, t, :], bankL[:, t, :], ACT.Exp, bias=nrowmax[:, t:t + 1],
                                   accum_out=rowsum[:, nxt, t:t + 1]).then_inc(Ec_s, 1)

            def dispatch_weights(base, i):
                act.wait_ge(Ld_ps, i + (base + 2))
                act.activation(E_d[:, :, :], bankL[:, :, :], ACT.Exp).then_inc(Ed_s, 1)

            def body1(i, par, has):
                if has(0):
                    second_half(0, i)
                if has(1):
                    combine_weights(0, i, 1 - par)
                if has(-2):
                    act.wait_ge(mT_ps, i - 1)
                    act.activation(mT[:, :], bankH[:, 0, :], ACT.Copy).then_inc(mT_s, 1)
                if has(1):
                    dispatch_weights(0, i)
                if has(-2):
                    uz = bankM[:, 0, :].rearrange("p (h r c) -> p h r c", h=2, r=2)
                    act.wait_ge(uz_ps, i - 1)
                    act.activation(u_part(0, i - 2), uz[:, :, 0, :], ACT.Copy).then_inc(uh_s, 1)
                    if has(-3):
                        act.wait_ge(e1_s, i - 2)
                    act.activation(sig[:, :, :], uz[:, :, 1, :], ACT.Exp, scale=-1.0).then_inc(e_s, 1)
                    act.activation(z[:, :, bass.ds(i - 2, 1), :].rearrange("p h o c -> p h (o c)"), uz[:, :, 1, :],
                                   ACT.Copy).then_inc(zc_s, 1)

            def body2(i, par, has):
                if has(0):
                    second_half(NB, i)
                if has(1):
                    combine_weights(NB, i, 1 - par)
                if has(4):
                    act.wait_ge(ygT_ps, i + 5)
                    act.activation(mT[:, 0:SEQ], bankH[:, 0, 0:SEQ], ACT.Copy).then_inc(ygT_s, 1)
                if has(1):
                    dispatch_weights(NB, i)

            steps(act, body1, **FFN1)

            act.sem_inc(y_s, RING)

            def take_y(c, s, j):
                act.wait_ge(conv_ps, c + 1)
                act.activation(y_of(c * CH, CH), conv_bank(s), ACT.Copy).then_inc(y_s, 1)
            conv_rounds(act, take_y)
            steps(act, body2, **FFN2)

        @block.vector
        def _(dve):
            count = [0]

            def link(ins):
                count[0] += 1
                ins.then_inc(dve_seq, 1)
                dve.wait_ge(dve_seq, count[0])

            for h in range(2):
                e = dve.memset(xn[:, h, :, D:D + 1], 1.0)
            dve.wait_ge(w_se, 48)
            link(dve.tensor_tensor(gslot[:, :], gslot[:, :], gxrow[:, :], ALU.mult))
            dve.tensor_tensor(se_n[:, :, :], raw_se[:, :, :],
                              gslot[:, :].unsqueeze(1).to_broadcast([P, ST, D]), ALU.mult).then_inc(se_row, 1)
            dve.wait_ge(se_sum, 1)
            dve.tensor_scalar(ms[:, :], ss[:, :], 1.0 / D, RMS_EPS * RMS_EPS / D, ALU.mult, ALU.max).then_inc(se_floor, 1)

            def slots_scale():
                dve.wait_ge(se_row, 1)
                dve.wait_ge(se_scale, 1)
                for s in range(ST):
                    e = dve.tensor_scalar(se_n[:, s, :], se_n[:, s, :], sef[:, s:s + 1], None, ALU.mult)
                e.then_inc(se_row, 1)

            def slots_parts():
                dve.wait_ge(seT_ps, 1)
                link(dve.tensor_copy(seh[:, :], bankH[:, 0, :]))
                dve.tensor_tensor(sel[:, :], bankH[:, 0, :], seh[:, :].bitcast(F32), ALU.subtract).then_inc(se_s, 1)

            def w1_parts():
                dve.wait_ge(w_w1, 32)
                dve.wait_ge(w1h_s, 1)
                link(dve.tensor_scalar(w1g[:, :], raw_w1[:, :], gxcol[:, 0:1], None, ALU.mult))
                dve.tensor_tensor(w1l[:, :], w1g[:, :], w1h[:, :].bitcast(F32), ALU.subtract).then_inc(w1_s, 1)

            def in_rows():
                dve.wait_ge(w_io, 112)
                link(dve.tensor_tensor(inw[:, :, :], raw_in[:, :, :],
                                       brow[:, :].unsqueeze(1).to_broadcast([P, 2, D]), ALU.mult))
                link(dve.reduce_sum(bias[:, :], inw[:, :, :], AX))
                link(dve.tensor_tensor(bias[:, :], bias[:, :], inb[:, :], ALU.add))
                link(dve.tensor_tensor(inw[:, :, :], raw_in[:, :, :],
                                       grow[:, :].unsqueeze(1).to_broadcast([P, 2, D]), ALU.mult))
                link(dve.tensor_tensor(insq[:, 0, :], inw[:, 0, :], inw[:, 0, :], ALU.mult))
                link(dve.reduce_sum(n2[:, :], insq[:, 0, :], AX))
                dve.tensor_scalar(n2[:, :], n2[:, :], float(D) * 1.01, 1e-30, ALU.mult, ALU.max).then_inc(n2_s, 1)

            def in_scale():
                dve.wait_ge(n2_s, 1)
                dve.wait_ge(nrm_s, 1)
                link(dve.tensor_scalar(nbias[:, :], bias[:, 0:1], -1.0, None, ALU.mult))
                link(dve.tensor_tensor(nbias[:, :], bias[:, 0:1], nbias[:, :], ALU.max))
                link(dve.scalar_tensor_tensor(out=ubound[:, :], in0=n2[:, :], scalar=nrm[:, 0:1], in1=nbias[:, :],
                                              op0=ALU.mult, op1=ALU.add))
                link(dve.tensor_scalar(ubound[:, :], ubound[:, :], 1.0 / HALF, None, ALU.mult))
                link(dve.reciprocal(rub[:, :], ubound[:, :]))
                link(dve.tensor_scalar(inw[:, 0, :], inw[:, 0, :], rub[:, 0:1], None, ALU.mult))
                link(dve.tensor_scalar(bias[:, 0:1], bias[:, 0:1], rub[:, 0:1], None, ALU.mult))
                dve.wait_ge(cbs_s, 1)
                dve.tensor_scalar(oscale[:, :], ubound[:, :], cbs[:, 0:1], None, ALU.mult).then_inc(in_row, 1)

            def in_parts():
                dve.wait_ge(inT_ps, 1)
                link(dve.tensor_copy(inT[:, :], bankM[:, 0, 0:2 * D]))
                link(dve.tensor_scalar(outT[:, :], bankM[:, 0, 2 * D:3 * D], oscale[:, 0:1], None, ALU.mult))
                link(dve.tensor_copy(brep[:, :], bankH[:, 0, 0:2 * D]))
                link(dve.tensor_copy(binh[:, :], brep[:, :]))
                link(dve.tensor_tensor(brep[:, :], brep[:, :], binh[:, :].bitcast(F32), ALU.subtract))
                link(dve.tensor_copy(binh[64:P, :], brep[64:P, :]))
                link(dve.memset(brep[:, 0:P], 0.0))
                link(dve.memset(brep[0:1, 0:P], 1.0))
                link(dve.memset(brep[64:65, 0:P], 1.0))
                dve.tensor_copy(oneh[:, :], brep[:, 0:P]).then_inc(mix_set, 1)

            def ffn_body(base, i, par, has):
                first = base == 0
                nxt = 1 - par
                if has(0):
                    dve.wait_ge(sTh_s, i + (base + 1))
                    dve.tensor_tensor(sTl[:, :], bankM[:, 0, :], sTh[:, :].bitcast(F32), ALU.subtract).then_inc(sT_s, 1)
                if has(1):
                    if first and has(-1):
                        dve.wait_ge(x_s, i)
                    if not first and has(3):
                        dve.wait_ge(mixed, i + 4)
                    dve.wait_ge(LT_ps, i + (base + 2))
                    dve.reduce_max(colmax[:, :], LT, AX).then_inc(cmax_s, 1)
                    dve.wait_ge(L_ps, i + (base + 2))
                    dve.reduce_max(rowmax[:, :], bankL[:, :, :], AX).then_inc(rmax_s, 1)
                    dve.wait_ge(rmax_s, i + (base + 2))
                    dve.tensor_scalar(nrowmax[:, :], rowmax[:, :], -1.0, None, ALU.mult).then_inc(nrmax_s, 1)
                    dve.wait_ge(cmax_s, i + (base + 2))
                    dve.tensor_scalar(ncolmax[:, :], colmax[:, :], -1.0, None, ALU.mult).then_inc(ncmax_s, 1)
                elif first and has(-1):
                    dve.wait_ge(x_s, i)
                elif not first and has(3):
                    dve.wait_ge(mixed, i + 4)
                if first and i_is(i, -2):
                    slots_scale()
                if has(2):
                    dve.wait_ge(xT_ps, i + (base + 3))
                    dve.tensor_copy(xTh[:, par, :], bankM[:, 1, 0:SEQ]).then_inc(xTh_s, 1)
                    dve.wait_ge(xTh_s, i + (base + 3))
                    dve.tensor_tensor(xTl[:, par, :], bankM[:, 1, 0:SEQ], xTh[:, par, :].bitcast(F32),
                                      ALU.subtract).then_inc(xT_s, 1)
                if first and i_is(i, -2):
                    slots_parts()
                if first and i_is(i, -1):
                    w1_parts()
                if not first and has(4):
                    y = u32[:, :, :].rearrange("p c (h b) -> p h c b", h=2)[:, :, :, bass.ds(i + 4, 1)]
                    dve.tensor_tensor(yg[:, :, :], y.rearrange("p h c o -> p h (c o)"),
                                      z[:, :, bass.ds(i + 4, 1), :].rearrange("p h o c -> p h (o c)"),
                                      ALU.mult).then_inc(yg_s, 1)
                if has(3):
                    if first and type(i) is int and (i + 3) % XB == 0:
                        dve.wait_ge(x_in_s[(i + 3) // XB], 16)
                    if first and i_is(i, 2):
                        for c in range((i + 3) // XB + 1, XCH):
                            dve.wait_ge(x_in_s[c], 16)
                    for t in range(TT):
                        e = dve.bn_stats(bn6[:, t, :], tile((i + 3) * TT + t).rearrange("p o d -> p (o d)"))
                    e.then_inc(bn_s, 1)
                again = first and has(-1)
                if again:
                    for t in range(TT):
                        e = dve.bn_stats(bnm[:, t, :], tile((i - 1) * TT + t).rearrange("p o d -> p (o d)"))
                    e.then_inc(mbn_s, 1)
                if first and has(-3):
                    z_b = z[:, :, bass.ds(i - 3, 1), :].rearrange("p h o c -> p h (o c)")
                    dve.wait_ge(e_s, i - 2)
                    dve.tensor_scalar(upd[:, :, :], sig[:, :, :], 1.0, None, ALU.add).then_inc(e1_s, 1)
                    dve.wait_ge(e1_s, i - 2)
                    dve.reciprocal(rsig[:, :, :], upd[:, :, :]).then_inc(sig_s, 1)
                    dve.wait_ge(sig_s, i - 2)
                    dve.wait_ge(zc_s, i - 2)
                    dve.tensor_tensor(z_b, z_b, rsig[:, :, :], ALU.mult).then_inc(z_s, 1)
                if has(3):
                    dve.wait_ge(bn_s, i + (base + 4))
                if again:
                    dve.wait_ge(mbn_s, i)
                if has(0):
                    dve.wait_ge(proc_ps, i + (base + 1))
                    dve.tensor_copy(proc[:, :, :].rearrange("p s d -> p (s d)"), bankH[:, 1, :]).then_inc(proc_s, 1)
                if has(3):
                    for t in range(TT):
                        e = dve.bn_aggr(mean_var[:, nxt, t, :], bn6[:, t, :])
                    e.then_inc(mv_s, 1)
                if again:
                    for t in range(TT):
                        e = dve.bn_aggr(new_mv[:, t, :], bnm[:, t, :])
                    e.then_inc(mag_s, 1)
                if has(1):
                    dve.wait_ge(EcT_ps, i + (base + 2))
                    dve.tensor_copy(E_cT[:, nxt, :, :], LT).then_inc(EcT_s, 1)
                if has(3):
                    dve.wait_ge(mv_s, i + (base + 4))
                    dve.tensor_scalar(floor_var[:, nxt, :], mean_var[:, nxt, :, 1],
                                      LN_EPS * RMS_EPS * RMS_EPS / D, None, ALU.max).then_inc(var_s, 1)
                if again:
                    dve.wait_ge(mag_s, i)
                    dve.tensor_scalar(mix_var[:, 0, nxt, :], new_mv[:, :, 1], 1.0 + LN_EPS, LN_EPS * LN_EPS,
                                      ALU.mult, ALU.add)
                    dve.tensor_scalar(mix_var[:, 1, nxt, :], new_mv[:, :, 1], LN_EPS, None, ALU.add).then_inc(mvar_s, 1)
                    dve.tensor_scalar(nmean[:, bass.ds((i - 1) * TT, TT)], new_mv[:, :, 0], -1.0, None, ALU.mult)\
                       .then_inc(mvar_s, 1)
                if first and i_is(i, 1):
                    in_parts()
                if first and has(-2):
                    uz = bankM[:, 0, :].rearrange("p (h r c) -> p h r c", h=2, r=2)
                    dve.wait_ge(uh_s, i - 1)
                    dve.wait_ge(zc_s, i - 1)
                    dve.tensor_tensor(u_part(1, i - 2), uz[:, :, 0, :], u_part(0, i - 2), ALU.subtract).then_inc(u_s, 1)
                if not first and has(4):
                    dve.wait_ge(resb_s, i + 5)
                    dve.wait_ge(o_ps, i + 5)
                    dve.tensor_tensor(upd[:, :, :], bankM[:, 0, 0:SEQ].rearrange("p (h d) -> p h d", h=2),
                                      resb[:, :, :], ALU.add).then_inc(upd_s, 1)
                    dve.wait_ge(upd_s, i + 5)
                    dve.tensor_scalar(updc[:, :, :], upd[:, :, :], CLIP, -CLIP, ALU.min, ALU.max).then_inc(updc_s, 1)
                    dve.wait_ge(updc_s, i + 5)
                    dve.tensor_tensor(tile((i + 4) * TT, TT), tile((i + 4) * TT, TT), updc[:, :, :], ALU.add)\
                       .then_inc(mixed, 1)
                if has(1):
                    dve.reciprocal(rrow[:, :], rowsum[:, nxt, :]).then_inc(rrow_s, 1)
                    dve.wait_ge(rrow_s, i + (base + 2))
                    dve.tensor_scalar(hrrow[:, nxt, :], rrow[:, :], 0.5, None, ALU.mult).then_inc(hrrow_s, 1)
                    dve.wait_ge(slots_ps, i + (base + 2))
                    dve.reciprocal(rslot[:, :, :], slot_ps[:, :, :, D]).then_inc(rslot_s, 1)
                    dve.wait_ge(rslot_s, i + (base + 2))
                    dve.tensor_tensor(slots_n[:, :, :].rearrange("p (a s) d -> p a s d", a=2), slot_ps[:, :, :, 0:D],
                                      rslot[:, :, :].unsqueeze(3).to_broadcast([P, 2, 2, D]), ALU.mult)\
                       .then_inc(slots_s, 1)
                if has(3):
                    dve.wait_ge(scale_s, i + (base + 4))
                    for t in range(TT):
                        e = dve.tensor_scalar(xn[:, nxt, t, 0:D].unsqueeze(1), tile((i + 3) * TT + t),
                                              mean_var[:, nxt, t, 0:1], scale_x[:, nxt, t:t + 1],
                                              ALU.subtract, ALU.mult)
                    e.then_inc(xn_s, 1)
                if has(0):
                    dve.wait_ge(hrrow_s, i + (base + 1))
                    dve.wait_ge(out_ps, i + (base + 1))
                    for t in range(TT):
                        n = i * TT + t
                        e = dve.scalar_tensor_tensor(out=tile(n), in0=bankM[:, 1, t * D:(t + 1) * D].unsqueeze(1),
                                                     scalar=hrrow[:, par, t:t + 1], in1=tile(n),
                                                     op0=ALU.mult, op1=ALU.add)
                    e.then_inc(x_s, 1)
                if first and i_is(i, -1):
                    in_rows()
                if first and i_is(i, 0):
                    in_scale()

            steps(dve, lambda i, par, has: ffn_body(0, i, par, has), **FFN1)
            dve.wait_ge(z_s, NB)
            dve.wait_ge(y_s, NCH + RING)
            steps(dve, lambda i, par, has: ffn_body(NB, i, par, has), **FFN2)

        @block.tensor
        def _(pe):
            def combine(par, t):
                for s in range(ST):
                    e = pe.matmul(bankM[:, 1, t * D:(t + 1) * D], E_cT[:, par, s, t * P:(t + 1) * P], proc[:, s, :],
                                  start=(s == 0), stop=(s == ST - 1))
                return e

            def set_up_slots():
                pe.wait_ge(se_row, 2)
                for s in range(ST):
                    e = pe.transpose(bankH[:, 0, s * P:(s + 1) * P], se_n[:, s, :], ident[:, :])
                e.then_inc(seT_ps, 1)

            def set_up_mixer():
                pe.wait_ge(in_row, 1)
                pe.wait_ge(w_io, 112)
                for r in range(2):
                    pe.transpose(bankM[:, 0, r * D:(r + 1) * D], inw[:, r, :], ident[:, :])
                    pe.matmul(bankH[:, 0, r * D:(r + 1) * D], bias[:, r:r + 1].to_broadcast([P, P]), ident[:, :],
                              start=True, stop=True)
                pe.transpose(bankM[:, 0, 2 * D:3 * D], raw_out[:, :], ident[:, :]).then_inc(inT_ps, 1)

            def ffn_body(base, i, par, has):
                first = base == 0
                nxt = 1 - par
                side = has(-2) if first else has(4)
                n_side = i - 1 if first else i + 5
                if has(1):
                    pe.wait_ge(xT_s, i + (base + 2))
                    if first and i_is(i, -1):
                        pe.wait_ge(se_s, 1)
                    if has(0):
                        pe.wait_ge(EcT_s, i + (base + 1))
                    for s in range(ST):
                        e = pe.matmul(LT[:, s, :], seh[:, s * P:(s + 1) * P], xTh[:, nxt, :], start=True, stop=True)
                    e.then_inc(LT_ps, 1)
                if has(0):
                    pe.wait_ge(slots_s, i + (base + 1))
                    if first and i_is(i, 2):
                        pe.wait_ge(mix_set, 1)
                    if first and has(-3):
                        pe.wait_ge(u_s, i - 2)
                    if not first:
                        pe.wait_ge(upd_s, min(i + 4, NB) if type(i) is int else i + 4)
                    for s in range(ST):
                        e = pe.transpose(bankM[:, 0, s * P:(s + 1) * P], slots_n[:, s, :], ident[:, :])
                    e.then_inc(sT_ps, 1)
                if has(1):
                    for t in range(TT):
                        e = split3(pe, bankL[:, t, :], xTh[:, nxt, t * P:(t + 1) * P], xTl[:, nxt, t * P:(t + 1) * P],
                                   seh[:, :], sel[:, :])
                    e.then_inc(L_ps, 1)
                if has(2):
                    pe.wait_ge(xn_s, i + (base + 3))
                    if has(-1):
                        pe.wait_ge(x_s, i + base)
                    if has(1):
                        pe.wait_ge(xT_s, i + (base + 2))
                    for t in range(TT):
                        e = pe.transpose(bankM[:, 1, t * P:(t + 1) * P], xn[:, par, t, 0:D], ident[:, :])
                    e.then_inc(xT_ps, 1)
                if first and i_is(i, -2):
                    set_up_slots()
                if has(0):
                    pe.wait_ge(sT_s, i + (base + 1))
                    if first and i_is(i, 0):
                        pe.wait_ge(w1_s, 1)
                        pe.wait_ge(w_w2, 16)
                    for k in range(HT):
                        if k == 3:
                            pe.wait_ge(gelu_s, i * HT + (base * HT + 1))
                        split3(pe, h_bank(k), w1h[:, k * P:(k + 1) * P], w1l[:, k * P:(k + 1) * P],
                               sTh[:, :], sTl[:, :]).then_inc(h_ps, 1)
                    for k in range(2):
                        pe.wait_ge(gelu_s, i * HT + (base * HT + 2 + k))
                        project(k)
                if side:
                    if has(0):
                        pe.wait_ge(gelu_s, i * HT + (base * HT + HT))
                    if first:
                        pe.wait_ge(xm_s, n_side)
                        for t in range(TT):
                            pe.transpose(bankH[:, 0, t * P:(t + 1) * P], xm[:, t, :], ident[:, :])
                            e = pe.transpose(bankH[:, 0, SEQ + t * P:SEQ + (t + 1) * P], xm[:, t, :], flip[:, :])
                        e.then_inc(mT_ps, 1)
                    else:
                        pe.wait_ge(yg_s, n_side)
                        for t in range(TT):
                            e = pe.transpose(bankH[:, 0, t * P:(t + 1) * P], yg[:, t, :], ident[:, :])
                        e.then_inc(ygT_ps, 1)
                if has(0):
                    pe.wait_ge(gelu_s, i * HT + (base * HT + HT))
                    project(2)
                    project(3).then_inc(proc_ps, 1)
                if has(1):
                    pe.wait_ge(Ec_s, i * TT + ((base + 2) * TT))
                    pe.wait_ge(ncmax_s, i + (base + 2))
                    for t in range(TT):
                        for s in range(ST):
                            e = pe.matmul(bankL[:, t, s * P:(s + 1) * P], ncolmax[:, s:s + 1].to_broadcast([P, P]),
                                          identb[:, :], start=False, stop=True, skip_group_check=True)
                    e.then_inc(Ld_ps, 1)
                    for s in range(ST):
                        for t in range(TT):
                            e = pe.transpose(LT[:, s, t * P:(t + 1) * P], E_c[:, t, s * P:(s + 1) * P], ident[:, :])
                    e.then_inc(EcT_ps, 1)
                if first and i_is(i, 1):
                    set_up_mixer()
                if side and first:
                    pe.wait_ge(mT_s, n_side)
                    if not has(0):
                        pe.wait_ge(u_s, i - 2)
                    for t in range(TT):
                        dst = bankM[:, 0, t * 2 * D:(t + 1) * 2 * D]
                        pe.matmul(dst, oneh[:, :], binh[:, :], start=True, stop=False, skip_group_check=True)
                        pe.matmul(dst[:, 0:D], mT[:, SEQ + t * P:SEQ + (t + 1) * P], inT[:, 0:D],
                                  start=False, stop=True, skip_group_check=True)
                        e = pe.matmul(dst[:, D:2 * D], mT[:, t * P:(t + 1) * P], inT[:, D:2 * D],
                                      start=False, stop=True, skip_group_check=True)
                    e.then_inc(uz_ps, 1)
                if side and not first:
                    pe.wait_ge(ygT_s, n_side)
                    if not has(0) and has(3):
                        pe.wait_ge(upd_s, i + 4)
                    for t in range(TT):
                        e = pe.matmul(bankM[:, 0, t * D:(t + 1) * D], mT[:, t * P:(t + 1) * P], outT[:, :],
                                      start=True, stop=True)
                    e.then_inc(o_ps, 1)
                if has(0):
                    pe.wait_ge(proc_s, i + (base + 1))
                    if has(2):
                        pe.wait_ge(xT_s, i + (base + 3))
                    combine(par, 0)
                if has(1):
                    pe.wait_ge(Ed_s, i + (base + 2))
                    if first and i_is(i, 1):
                        pe.wait_ge(mix_set, 1)
                    if side:
                        pe.wait_ge(mT_s if first else ygT_s, n_side)
                    for s in range(ST):
                        for t in range(TT):
                            e = pe.matmul(slot_ps[:, s // 2, s % 2, 0:D + 1], E_d[:, t, s * P:(s + 1) * P],
                                          xn[:, nxt, t, :], start=(t == 0), stop=(t == TT - 1))
                    e.then_inc(slots_ps, 1)
                if has(0):
                    combine(par, 1).then_inc(out_ps, 1)

            def project(k):
                for s in range(ST):
                    e = pe.matmul(bankH[:, 1, s * D:(s + 1) * D], hT[:, k, s * P:(s + 1) * P], w2s[:, k, :],
                                  start=(k == 0 and s == 0), stop=(k == HT - 1), skip_group_check=True)
                return e

            pe.wait_ge(consts, 10)
            steps(pe, lambda i, par, has: ffn_body(0, i, par, has), **FFN1)

            pe.wait_ge(u_s, NB)
            pe.wait_ge(x_s, NB)

            def convolve(g, s, j):
                pe.wait_ge(toep_s[s], j * 32 + 32)
                pe.wait_ge(y_s, g + 1)
                for c in range(CH):
                    dst = conv_bank(s)[:, c, :]
                    uc = u[:, bass.ds(g * CH + c, 1), :, :]
                    uh = uc[:, :, 0, :].rearrange("p o n -> p (o n)")
                    ul = uc[:, :, 1, :].rearrange("p o n -> p (o n)")
                    near = [toeplitz(s, c, part, 0) for part in range(2)]
                    far = [toeplitz(s, c, part, P) for part in range(2)]
                    pe.matmul(dst, near[0], uh, start=True, stop=False, skip_group_check=True)
                    pe.matmul(dst, near[0], ul, start=False, stop=False, skip_group_check=True)
                    pe.matmul(dst, near[1], uh, start=False, stop=False, skip_group_check=True)
                    pe.matmul(dst[:, NB:], far[0], uh[:, 0:NB], start=False, stop=False, skip_group_check=True)
                    pe.matmul(dst[:, NB:], far[0], ul[:, 0:NB], start=False, stop=False, skip_group_check=True)
                    e = pe.matmul(dst[:, NB:], far[1], uh[:, 0:NB], start=False, stop=True, skip_group_check=True)
                e.then_inc(conv_ps, 1)
            conv_rounds(pe, convolve)
            steps(pe, lambda i, par, has: ffn_body(NB, i, par, has), **FFN2)


_INS = ['L0_attn_x', 'L0_attn_A_log', 'L0_attn_B_param', 'L0_attn_C_param', 'L0_attn_log_dt', 'L0_attn_in_w',
        'L0_attn_in_b', 'L0_attn_out_w', 'L0_attn_out_b', 'L0_attn_ln_g', 'L0_attn_ln_b', 'L0_ffn_gamma_x',
        'L0_ffn_gamma_slot', 'L0_ffn_slot_embeds', 'L0_ffn_w1', 'L0_ffn_w2']


def kernel(**inputs):
    import numpy as _np
    import concourse.bacc as _bacc
    from concourse import mybir as _mybir
    from concourse.bass_utils import run_bass_kernel_spmd as _run

    nc = _bacc.Bacc("TRN2", target_bir_lowering=False, num_devices=1)
    arrays, args = {}, []
    for name in _INS:
        a = _np.ascontiguousarray(inputs[name])
        arrays[f"in_{name}"] = a
        args.append(nc.dram_tensor(f"in_{name}", a.shape, _mybir.dt.from_np(a.dtype), kind="ExternalInput").ap())
    args.append(nc.dram_tensor("out_x", inputs['L0_attn_x'].shape, _mybir.dt.from_np(_np.dtype("float32")),
                               kind="ExternalOutput").ap())
    macaron_kernel(nc, *args)
    return _run(nc, [arrays], core_ids=[0]).results[0]["out_x"]
```

```python
import math
from contextlib import ExitStack

import concourse.bass as bass
from concourse import mybir

F32 = mybir.dt.float32
F32R = mybir.dt.float32r
F16 = mybir.dt.float16
BF16 = mybir.dt.bfloat16
ALU = mybir.AluOpType
ACT = mybir.ActivationFunctionType
AX = mybir.AxisListType.X

P = 128
LN_EPS = 1e-5
RMS_EPS = 1e-12
LOG_A_MIN = math.log(1e-8)
DT_MIN, DT_MAX = 1e-4, 1.0
CLIP = 10.0
HALF = 4096.0
WIDE = 32768.0
SHIFT = math.log(HALF)
ROUND = 2.0 ** -8


def macaron_kernel(nc, x_in, A_log, B_param, C_param, log_dt, in_w, in_b, out_w, out_b,
                   ln_g, ln_b, gamma_x, gamma_slot, slot_embeds, w1, w2, out):
    NB, SEQ, D = x_in.shape
    TT = SEQ // P
    NT = NB * TT
    NS = A_log.shape[1]
    SLOTS = slot_embeds.shape[0] * slot_embeds.shape[1]
    ST = SLOTS // P
    HID = w1.shape[1]
    HT = HID // P
    assert D == P and TT == 2 and ST == 4 and HT == 4 and NB % 2 == 0

    CH = 8
    NCH = D // CH
    RING = 8
    EARLY = 5
    LAG0 = SEQ // 2 - 1
    KP = 384
    XCH = 8
    XB = NB // XCH

    x_dram = x_in.rearrange("b (h p) d -> p (b h) d", p=P)
    out_dram = out.rearrange("b (h p) d -> p (b h) d", p=P)
    resp_dram = nc.dram_tensor("resp_dram", [D, 2, KP], F16, kind="Internal")

    ctx = ExitStack()
    with ctx:
        def sb(name, shape, dt=F32, where=ctx):
            return where.enter_context(nc.sbuf_tensor(name, shape, dt))

        def psum(name, shape):
            return ctx.enter_context(nc.psum_tensor(name, shape, F32))

        def sem(name):
            return ctx.enter_context(nc.semaphore(name))

        x = sb("x", [P, NT, D])
        ident = sb("ident", [P, P])
        identb = sb("identb", [P, P], BF16)
        flip = sb("flip", [P, P])
        w1h = sb("w1h", [P, HID], F32R)
        w1l = sb("w1l", [P, HID], F32R)
        w2s = sb("w2s", [P, HT, D])
        seh = sb("seh", [P, SLOTS], F32R)
        sel = sb("sel", [P, SLOTS], F32R)
        inT = sb("inT", [P, 2 * D])
        binh = sb("binh", [P, 2 * D], F32R)
        oneh = sb("oneh", [P, P], F32R)
        outT = sb("outT", [P, D])
        obias = sb("obias", [P, D])
        respp = sb("respp", [P, 2, KP], F16)
        mean_var = sb("mean_var", [P, 2, TT, 2])
        floor_var = sb("floor_var", [P, 2, TT])
        scale_x = sb("scale_x", [P, 2, TT])
        new_mv = sb("new_mv", [P, TT, 2])
        mix_var = sb("mix_var", [P, 2, 2, TT])
        mix_scale = sb("mix_scale", [P, 2, TT])
        res2 = sb("res2", [P, TT, D])
        nmean = sb("nmean", [P, NT])
        rstd = sb("rstd", [P, NT])
        mhalf = sb("mhalf", [P, ST])
        bn6 = sb("bn6", [P, 2, 6])
        bnm = sb("bnm", [P, 2, 6])
        u = sb("u", [P, D, 2, 2 * NB], F16)
        z = sb("z", [P, 2, NB, D])
        xm = sb("xm", [P, TT, D])
        xc = sb("xc", [P, TT, D])
        mT = sb("mT", [P, 2 * SEQ])
        upd = sb("upd", [P, TT, D])
        sig = sb("sig", [P, TT, D])
        rsig = sb("rsig", [P, TT, D])

        xn = sb("xn", [P, 2, TT, D], F32)
        xnh = sb("xnh", [P, 2, TT, D + 1], F16)
        xnl = sb("xnl", [P, 2, TT, D], F16)
        xTh = sb("xTh", [P, 2, SEQ], F32R)
        xTl = sb("xTl", [P, 2, SEQ], F32R)
        E_c = sb("E_c", [P, TT, SLOTS], F32)
        slots_n = sb("slots_n", [P, ST, D], F32)
        sTh = sb("sTh", [P, SLOTS], F32R)
        sTl = sb("sTl", [P, SLOTS], F32R)
        proch = sb("proch", [P, ST, D], F16)
        procl = sb("procl", [P, ST, D], F16)
        zero = sb("zero", [P, TT])
        cscale = sb("cscale", [P, 1])
        colmax = sb("colmax", [P, ST], F32)
        ncolmax = sb("ncolmax", [P, ST], BF16)
        ncm = sb("ncm", [P, 2, ST], F32)
        rowmax = sb("rowmax", [P, TT], F32)
        nrowmax = sb("nrowmax", [P, TT], F32)
        rowsum = sb("rowsum", [P, 2, TT], F32)
        rrow = sb("rrow", [P, TT], F32)
        hrrow = sb("hrrow", [P, 2, TT], F32)
        rslot = sb("rslot", [P, 2, 2], F32)
        ffn = ExitStack()
        E_d = sb("E_d", [P, TT, SLOTS], F32, ffn)
        E_dh = sb("E_dh", [P, TT, SLOTS], F16, ffn)
        E_dl = sb("E_dl", [P, TT, SLOTS], F16, ffn)
        E_cTh = sb("E_cTh", [P, 2, ST, SEQ], F16, ffn)
        E_cTl = sb("E_cTl", [P, 2, ST, SEQ], F16, ffn)
        hT = sb("hT", [P, HT, SLOTS], F32, ffn)
        ffn.close()
        toep_late = sb("toep_late", [P, RING - EARLY, CH, 2, SEQ], F16)
        setup = ExitStack()
        raw_w1 = sb("raw_w1", [P, HID], F32, setup)
        raw_se = sb("raw_se", [P, ST, D], F32, setup)
        raw_in = sb("raw_in", [P, 2, D], F32, setup)
        raw_out = sb("raw_out", [P, D], F32, setup)
        gslot = sb("gslot", [P, D], F32, setup)
        gxrow = sb("gxrow", [P, D], F32, setup)
        grow = sb("grow", [P, D], F32, setup)
        brow = sb("brow", [P, D], F32, setup)
        gxcol = sb("gxcol", [P, 1], F32, setup)
        inb = sb("inb", [P, 2], F32, setup)
        Alog = sb("Alog", [P, NS], F32, setup)
        Bp = sb("Bp", [P, NS], F32, setup)
        Cp = sb("Cp", [P, NS], F32, setup)
        ldt = sb("ldt", [P, 1], F32, setup)
        mone = sb("mone", [P, 1], F32, setup)
        raw_w2 = sb("raw_w2", [P, HT, D], F32, setup)
        w1sq = sb("w1sq", [P, HID], F32, setup)
        w2sq = sb("w2sq", [P, HT, D], F32, setup)
        w1sum = sb("w1sum", [P, 1], F32, setup)
        ones = sb("ones", [P, P], F32, setup)
        w2max = sb("w2max", [P, 1], F32, setup)
        b2 = sb("b2", [P, 1], F32, setup)
        rb = sb("rb", [P, 1], F32, setup)
        bscale = sb("bscale", [P, 1], F32, setup)
        sq = sb("sq", [P, ST, D], F32, setup)
        ss = sb("ss", [P, ST], F32, setup)
        ms = sb("ms", [P, ST], F32, setup)
        sef = sb("sef", [P, ST], F32, setup)
        se_n = sb("se_n", [P, ST, D], F32, setup)
        w1g = sb("w1g", [P, HID], F32, setup)
        lags = sb("lags", [P, SEQ], F32, setup)
        half = sb("half", [P, NS], F32, setup)
        powers = sb("powers", [P, NS, SEQ], F32, setup)
        resp = sb("resp", [P, SEQ], F32, setup)
        expA = sb("expA", [P, NS], F32, setup)
        expdt = sb("expdt", [P, 1], F32, setup)
        dt = sb("dt", [P, 1], F32, setup)
        logA = sb("logA", [P, NS], F32, setup)
        cb = sb("cb", [P, NS], F32, setup)
        cbn = sb("cbn", [P, NS], F32, setup)
        cbs = sb("cbs", [P, 1], F32, setup)
        rcbs = sb("rcbs", [P, 1], F32, setup)
        inw = sb("inw", [P, 2, D], F32, setup)
        insq = sb("insq", [P, 2, D], F32, setup)
        bias = sb("bias", [P, 2], F32, setup)
        n2 = sb("n2", [P, 1], F32, setup)
        nrm = sb("nrm", [P, 1], F32, setup)
        ubound = sb("ubound", [P, 1], F32, setup)
        rub = sb("rub", [P, 1], F32, setup)
        nbias = sb("nbias", [P, 1], F32, setup)
        oscale = sb("oscale", [P, 1], F32, setup)
        brep = sb("brep", [P, 2 * D], F32, setup)
        setup.close()
        toep_early = sb("toep_early", [P, EARLY, CH, 2, SEQ], F16)
        res, resb, yg, updc = xc, xm, mT[:, SEQ:].rearrange("p (h d) -> p h d", h=TT), sig

        bankL = psum("bankL", [P, TT, SLOTS])
        bankT = psum("bankT", [P, 2, 512])
        bankH = psum("bankH", [P, 2, 512])
        bankM = psum("bankM", [P, 2, 512])
        LT = bankT[:, :, :].rearrange("p a (s t) -> p (a s) t", t=SEQ)
        SC = 130
        slot_ps = bankH[:, :, 0:2 * SC].rearrange("p a (s c) -> p a s c", c=SC)

        w_se, w_g, w_w1, w_w2, w_ssm, w_io = (sem(n) for n in ("w_se", "w_g", "w_w1", "w_w2", "w_ssm", "w_io"))
        x_in_s = [sem(f"x_in{c}") for c in range(XCH)]
        consts = sem("consts")
        dve_seq = sem("dve_seq")
        pool_seq = sem("pool_seq")
        se_sum, se_floor, se_scale, se_row = (sem(n) for n in ("se_sum", "se_floor", "se_scale", "se_row"))
        seT_ps, se_s, w1h_s, w1_s = (sem(n) for n in ("seT_ps", "se_s", "w1h_s", "w1_s"))
        wsum_s, bound_ps, b2_s, rb_s, w2_s = (sem(n) for n in ("wsum_s", "bound_ps", "b2_s", "rb_s", "w2_s"))
        Edh_s, Edl_s, xnp_s, ncm_s = (sem(n) for n in ("Edh_s", "Edl_s", "xnp_s", "ncm_s"))
        xnh_s = sem("xnh_s")
        bias_s, ones_s, rstd_s, EcTh_s, proch_s = (sem(n) for n in ("bias_s", "ones_s", "rstd_s", "EcTh_s", "proch_s"))
        n2_s, nrm_s, in_row, inT_ps, mix_set = (sem(n) for n in ("n2_s", "nrm_s", "in_row", "inT_ps", "mix_set"))
        ssm_exp, logA_s, powers_s, cbs_s = (sem(n) for n in ("ssm_exp", "logA_s", "powers_s", "cbs_s"))
        resp_s = sem("resp_s")
        resp_out = sem("resp_out")
        toep_s = [sem(f"toep{c}") for c in range(RING)]

        bn_s, mv_s, var_s, scale_s = (sem(n) for n in ("bn_s", "mv_s", "var_s", "scale_s"))
        mbn_s, mag_s, mvar_s = (sem(n) for n in ("mbn_s", "mag_s", "mvar_s"))
        xn_s, xT_ps, xTh_s, xT_s = (sem(n) for n in ("xn_s", "xT_ps", "xTh_s", "xT_s"))
        LT_ps, L_ps, Ld_ps = (sem(n) for n in ("LT_ps", "L_ps", "Ld_ps"))
        cmax_s, ncmax_s, rmax_s, nrmax_s = (sem(n) for n in ("cmax_s", "ncmax_s", "rmax_s", "nrmax_s"))
        Ec_s, Ed_s, EcT_ps, EcT_s = (sem(n) for n in ("Ec_s", "Ed_s", "EcT_ps", "EcT_s"))
        rrow_s, hrrow_s = sem("rrow_s"), sem("hrrow_s")
        slots_ps, rslot_s, slots_s = (sem(n) for n in ("slots_ps", "rslot_s", "slots_s"))
        sT_ps, sTh_s, sT_s = (sem(n) for n in ("sT_ps", "sTh_s", "sT_s"))
        h_ps, gelu_s, proc_ps, proc_s = (sem(n) for n in ("h_ps", "gelu_s", "proc_ps", "proc_s"))
        out_ps, x_s = sem("out_ps"), sem("x_s")

        mscale_s, xc_s, xm_s, mT_ps, mT_s = (sem(n) for n in ("mscale_s", "xc_s", "xm_s", "mT_ps", "mT_s"))
        uz_ps, e_s, zc_s, uh_s, u_s = (sem(n) for n in ("uz_ps", "e_s", "zc_s", "uh_s", "u_s"))
        e1_s, sig_s, z_s = (sem(n) for n in ("e1_s", "sig_s", "z_s"))
        conv_ps, y_s = sem("conv_ps"), sem("y_s")
        yg_s, ygT_ps, ygT_s, o_ps = (sem(n) for n in ("yg_s", "ygT_ps", "ygT_s", "o_ps"))
        rc_s, res_s, resb_s, upd_s, updc_s, mixed = (sem(n) for n in ("rc_s", "res_s", "resb_s", "upd_s", "updc_s", "mixed"))
        stored = sem("stored")

        block = ctx.enter_context(nc.Block())

        def steps(eng, body, first, loop_from, loop_to, last):
            for i in range(first, loop_from):
                body(i, i % 2, lambda k, i=i: 0 <= i + k < NB)
            with eng.Fori(0, (loop_to - loop_from) // 2, 1) as j:
                for p in range(2):
                    body(j * 2 + (loop_from + p), (loop_from + p) % 2, lambda k: True)
            for i in range(loop_to, last + 1):
                body(i, i % 2, lambda k, i=i: 0 <= i + k < NB)

        def h_bank(k):
            return (bankH[:, 0, :], bankH[:, 1, :], bankM[:, 0, :], bankH[:, 0, :])[k]

        def i_is(i, n):
            return type(i) is int and i == n

        def tile(t, n=1):
            return x[:, bass.ds(t, n), :]

        FFN1 = dict(first=-3, loop_from=3, loop_to=NB - 3, last=NB + 2)
        FFN2 = dict(first=-4, loop_from=2, loop_to=NB - 4, last=NB - 1)

        def split3(eng, out_ap, ah, al, bh, bl, stop=True, start=True):
            eng.matmul(out_ap, ah, bh, start=start, stop=False)
            eng.matmul(out_ap, ah, bl, start=False, stop=False)
            return eng.matmul(out_ap, al, bh, start=False, stop=stop)

        def toep_slot(s):
            return toep_early[:, s, :, :, :] if s < EARLY else toep_late[:, s - EARLY, :, :, :]

        def toeplitz(s, c, part, lag):
            return toep_slot(s)[:, c, part, lag:lag + P]

        def u_part(part, b):
            v = u[:, :, part, :].rearrange("p c (h b) -> p h c b", h=2)
            return v[:, :, :, bass.ds(b, 1)].rearrange("p h c o -> p h (c o)")

        u32 = u[:, :, :, :].rearrange("p c s n -> p (c s n)").bitcast(F32).rearrange("p (c n) -> p c n", n=2 * NB)

        def y_of(c, n):
            return u32[:, bass.ds(c, n), :]

        def conv_bank(s):
            b = (bankH, bankM, bankL, bankT)[s // 2]
            return b[:, s % 2, :].rearrange("p (c n) -> p c n", n=2 * NB)

        def conv_chunks(chunk):
            for g in range(NCH):
                chunk(g, g % RING)

        @block.sync
        def _(sp):
            sp.dma_start(raw_se[:, :, :], slot_embeds.rearrange("e t d -> (e t) d")
                         .rearrange("(s p) d -> p s d", p=P)).then_inc(w_se, 16)
            for c in range(XCH):
                sp.dma_start(x[:, c * XB * TT:(c + 1) * XB * TT, :],
                             x_dram[:, c * XB * TT:(c + 1) * XB * TT, :]).then_inc(x_in_s[c], 16)
                if c == 0:
                    sp.dma_start(raw_w1[:, :], w1).then_inc(w_w1, 16)
                    for dst, src in ((Alog, A_log), (Bp, B_param), (Cp, C_param)):
                        sp.dma_start(dst[:, :], src).then_inc(w_ssm, 16)
                    sp.dma_start(ldt[:, :], log_dt.rearrange("(d o) -> d o", o=1)).then_inc(w_ssm, 16)
                    sp.dma_start(raw_w2[:, :, :], w2.rearrange("(k p) d -> p k d", p=P)).then_inc(w_w2, 16)
                if c == 1:
                    sp.dma_start(raw_in[:, :, :], in_w.rearrange("(r p) d -> p r d", p=P)).then_inc(w_io, 16)
                    for r in range(2):
                        sp.dma_start(inb[:, r:r + 1], in_b[r * P:(r + 1) * P].rearrange("(p o) -> p o", o=1))\
                          .then_inc(w_io, 16)
                    sp.dma_start(grow[:, :], ln_g.partition_broadcast(P)).then_inc(w_io, 16)
                    sp.dma_start(brow[:, :], ln_b.partition_broadcast(P)).then_inc(w_io, 16)
                    sp.dma_start(raw_out[:, :], out_w).then_inc(w_io, 16)
                    sp.dma_start(obias[:, :], out_b.partition_broadcast(P)).then_inc(w_io, 16)
            sp.wait_ge(resp_s, 4)
            sp.dma_start(resp_dram[:, :, :], respp[:, :, :]).then_inc(resp_out, 16)
            sp.wait_ge(resp_out, 16)
            sp.wait_ge(mix_set, 1)
            for c in range(NCH):
                s = c % RING
                if c == EARLY:
                    sp.wait_ge(out_ps, NB)
                if c >= RING:
                    sp.wait_ge(conv_ps, c - RING + 1)
                for part in range(2):
                    src = bass.AP(resp_dram, c * CH * 2 * KP + part * KP,
                                  [[1, P], [2 * KP, CH], [1, SEQ]])
                    sp.dma_start(toep_slot(s)[:, :, part, :], src).then_inc(toep_s[s], 16)
            with sp.Fori(0, NB // 2, 1) as j:
                sp.wait_ge(x_s, j * 2 + (NB + 2))
                sp.dma_start(out_dram[:, bass.ds(j * 4, 4), :], x[:, bass.ds(j * 4, 4), :]).then_inc(stored, 16)
            sp.wait_ge(stored, 16 * (NB // 2))

        @block.gpsimd
        def _(pool):
            pool.memset(ident[:, :], 0.0).then_inc(consts, 1)
            pool.memset(identb[:, :], 0.0).then_inc(consts, 1)
            pool.memset(flip[:, :], 0.0).then_inc(consts, 1)
            pool.wait_ge(consts, 3)
            for m in (ident, identb):
                pool.affine_select(out=m[:, :], in_=m[:, :], compare_op=ALU.not_equal, fill=1.0, base=0,
                                   pattern=[[-1, P]], channel_multiplier=1).then_inc(consts, 1)
            pool.affine_select(out=flip[:, :], in_=flip[:, :], compare_op=ALU.not_equal, fill=1.0, base=1 - P,
                               pattern=[[1, P]], channel_multiplier=1).then_inc(consts, 1)
            pool.iota(lags[:, :], pattern=[[1, SEQ]], base=0, channel_multiplier=0,
                      allow_small_or_imprecise_dtypes=True).then_inc(consts, 1)
            pool.memset(mhalf[:, :], -0.5).then_inc(consts, 1)
            pool.memset(half[:, :], 0.5).then_inc(consts, 1)
            pool.memset(mone[:, :], -1.0).then_inc(consts, 1)
            pool.memset(zero[:, :], 0.0).then_inc(consts, 1)
            pool.wait_ge(consts, 11)
            count = [0]

            def link(ins):
                count[0] += 1
                ins.then_inc(pool_seq, 1)
                pool.wait_ge(pool_seq, count[0])

            pool.wait_ge(se_floor, 1)
            pool.tensor_tensor(sef[:, :], ms[:, :], mhalf[:, :], ALU.pow).then_inc(se_scale, 1)
            pool.wait_ge(ssm_exp, 2)
            link(pool.tensor_scalar(dt[:, :], expdt[:, :], DT_MIN, DT_MAX, ALU.max, ALU.min))
            link(pool.tensor_scalar(logA[:, :], expA[:, :], dt[:, 0:1], -1.0, ALU.mult, ALU.mult))
            pool.tensor_scalar(logA[:, :], logA[:, :], LOG_A_MIN, 0.0, ALU.max, ALU.min).then_inc(logA_s, 1)

            def gains():
                link(pool.tensor_tensor(cb[:, :], Bp[:, :], Cp[:, :], ALU.mult))
                link(pool.tensor_scalar(cb[:, :], cb[:, :], dt[:, 0:1], None, ALU.mult))
                link(pool.tensor_tensor(cbn[:, :], cb[:, :], cb[:, :], ALU.mult))
                link(pool.tensor_tensor(cbn[:, :], cbn[:, :], half[:, :], ALU.pow))
                n = NS // 2
                while n:
                    link(pool.tensor_tensor(cbn[:, 0:n], cbn[:, 0:n], cbn[:, n:2 * n], ALU.add))
                    n //= 2
                link(pool.tensor_scalar(cbs[:, :], cbn[:, 0:1], 1e-18, 1.01 / HALF, ALU.max, ALU.mult))
                link(pool.tensor_tensor(rcbs[:, :], cbs[:, :], mone[:, :], ALU.pow))
                pool.tensor_scalar(cb[:, :], cb[:, :], rcbs[:, 0:1], None, ALU.mult).then_inc(cbs_s, 1)
                pool.wait_ge(cbs_s, 1)

            def response(q):
                n = NS // 2
                pool.wait_ge(powers_s, (q + 1) * n)
                mine = powers[:, q * n:(q + 1) * n, :]
                link(pool.tensor_tensor(mine, mine, cb[:, q * n:(q + 1) * n].unsqueeze(2).to_broadcast([P, n, SEQ]),
                                        ALU.mult))
                while n > 1:
                    n //= 2
                    link(pool.tensor_tensor(mine[:, 0:n, :], mine[:, 0:n, :], mine[:, n:2 * n, :], ALU.add))
                if q == 1:
                    link(pool.tensor_tensor(resp[:, :], powers[:, 0, :], powers[:, NS // 2, :], ALU.add))

            def response_parts():
                pool.memset(respp[:, :, 0:LAG0], 0.0).then_inc(resp_s, 1)
                pool.memset(respp[:, :, LAG0 + SEQ:KP], 0.0).then_inc(resp_s, 1)
                pool.tensor_copy(respp[:, 0, LAG0:LAG0 + SEQ], resp[:, :]).then_inc(resp_s, 1)
                pool.wait_ge(resp_s, 3)
                pool.tensor_tensor(respp[:, 1, LAG0:LAG0 + SEQ], resp[:, :], respp[:, 0, LAG0:LAG0 + SEQ],
                                   ALU.subtract).then_inc(resp_s, 1)

            def centred(dst, b, done, value):
                t = b * TT
                pool.tensor_tensor(dst, tile(t, TT), nmean[:, bass.ds(t, TT)].unsqueeze(2).to_broadcast([P, TT, D]),
                                   ALU.add).then_inc(done, 1)
                pool.wait_ge(done, value)

            def ffn_scale(base, i, par, has):
                if has(3):
                    pool.wait_ge(var_s, i + (base + 4))
                    pool.tensor_tensor(scale_x[:, 1 - par, :], floor_var[:, 1 - par, :], mhalf[:, 0:TT], ALU.pow)\
                        .then_inc(scale_s, 1)

            def xn_parts(base, i, par, has):
                if has(3):
                    nxt = 1 - par
                    pool.wait_ge(xn_s, i + (base + 4))
                    if has(1):
                        pool.wait_ge(slots_ps, i + (base + 2))
                    pool.tensor_tensor(xnh[:, nxt, :, 0:D], xn[:, nxt, :, :],
                                       zero[:, :].unsqueeze(2).to_broadcast([P, TT, D]), ALU.add).then_inc(xnh_s, 1)
                    pool.wait_ge(xnh_s, i + (base + 4))
                    pool.tensor_tensor(xnl[:, nxt, :, :], xn[:, nxt, :, :], xnh[:, nxt, :, 0:D], ALU.subtract)\
                        .then_inc(xnp_s, 1)

            def body1(i, par, has):
                if has(-2):
                    pool.wait_ge(mscale_s, i - 1)
                    if has(-3):
                        pool.wait_ge(mT_ps, i - 2)
                    centred(xc[:, :, :], i - 2, xc_s, i - 1)
                    pool.tensor_tensor(xm[:, :, :], xc[:, :, :], mix_scale[:, par, :].unsqueeze(2).to_broadcast([P, TT, D]),
                                       ALU.mult).then_inc(xm_s, 1)
                ffn_scale(0, i, par, has)
                if has(-1):
                    pool.wait_ge(mvar_s, 2 * i)
                    pool.tensor_tensor(mix_scale[:, 1 - par, :], mix_var[:, 0, 1 - par, :], mhalf[:, 0:TT],
                                       ALU.pow).then_inc(mscale_s, 1)
                    pool.tensor_tensor(rstd[:, bass.ds((i - 1) * TT, TT)], mix_var[:, 1, 1 - par, :], mhalf[:, 0:TT],
                                       ALU.pow).then_inc(rstd_s, 1)
                if i_is(i, -2):
                    gains()
                if i_is(i, -1):
                    pool.wait_ge(b2_s, 1)
                    pool.tensor_tensor(rb[:, :], b2[:, :], mhalf[:, 0:1], ALU.pow).then_inc(rb_s, 1)
                if i_is(i, 0):
                    pool.wait_ge(n2_s, 1)
                    pool.tensor_tensor(nrm[:, :], n2[:, :], mhalf[:, 0:1], ALU.pow).then_inc(nrm_s, 1)
                for q in range(2):
                    if i_is(i, q):
                        response(q)
                if i_is(i, 2):
                    response_parts()
                xn_parts(0, i, par, has)

            def residual(i, has):
                c = i + 4
                if has(3):
                    pool.wait_ge(upd_s, c)
                centred(res[:, :, :], c, rc_s, i + 5)
                pool.tensor_tensor(res2[:, :, :], res[:, :, :],
                                   rstd[:, bass.ds(c * TT, TT)].unsqueeze(2).to_broadcast([P, TT, D]),
                                   ALU.mult).then_inc(res_s, 1)
                pool.wait_ge(res_s, i + 5)
                pool.tensor_tensor(resb[:, :, :], res2[:, :, :], obias[:, :].unsqueeze(1).to_broadcast([P, TT, D]),
                                   ALU.add).then_inc(resb_s, 1)

            def body2(i, par, has):
                if i_is(i, -4):
                    residual(i, has)
                    pool.wait_ge(z_s, NB)
                    pool.wait_ge(y_s, NCH + RING)
                if has(4):
                    if has(3):
                        pool.wait_ge(ygT_ps, i + 4)
                    y = u32[:, :, :].rearrange("p c (h b) -> p h c b", h=2)[:, :, :, bass.ds(i + 4, 1)]
                    pool.tensor_tensor(yg[:, :, :], y.rearrange("p h c o -> p h (c o)"),
                                       z[:, :, bass.ds(i + 4, 1), :].rearrange("p h o c -> p h (o c)"),
                                       ALU.mult).then_inc(yg_s, 1)
                    if not i_is(i, -4):
                        residual(i, has)
                ffn_scale(NB, i, par, has)
                xn_parts(NB, i, par, has)

            steps(pool, body1, **FFN1)
            pool.wait_ge(mT_ps, NB)
            pool.wait_ge(rstd_s, NB)
            steps(pool, body2, **FFN2)

        @block.scalar
        def _(act):
            act.dma_start(gslot[:, :], gamma_slot.partition_broadcast(P)).then_inc(w_g, 16)
            act.dma_start(gxrow[:, :], gamma_x.partition_broadcast(P)).then_inc(w_g, 16)
            act.dma_start(gxcol[:, :], gamma_x.rearrange("(d o) -> d o", o=1)).then_inc(w_w1, 16)
            act.wait_ge(w_se, 16)
            for s in range(ST):
                e = act.activation(sq[:, s, :], raw_se[:, s, :], ACT.Square, accum_out=ss[:, s:s + 1])
            e.then_inc(se_sum, 1)
            act.wait_ge(w_ssm, 64)
            act.activation(expA[:, :], Alog[:, :], ACT.Exp).then_inc(ssm_exp, 1)
            act.activation(expdt[:, :], ldt[:, :], ACT.Exp).then_inc(ssm_exp, 1)
            act.wait_ge(w_w1, 32)
            act.activation(w1h[:, :], raw_w1[:, :], ACT.Copy, scale=gxcol[:, 0:1]).then_inc(w1h_s, 1)
            act.activation(w1sq[:, :], raw_w1[:, :], ACT.Square, scale=gxcol[:, 0:1], accum_out=w1sum[:, :])\
               .then_inc(wsum_s, 1)
            act.wait_ge(w_w2, 16)
            act.activation(w2sq[:, :, :], raw_w2[:, :, :], ACT.Square).then_inc(wsum_s, 1)
            act.wait_ge(logA_s, 1)
            act.wait_ge(consts, 7)
            for n in range(NS):
                act.activation(powers[:, n, :], lags[:, :], ACT.Exp, scale=logA[:, n:n + 1]).then_inc(powers_s, 1)

            def second_half(base, i):
                act.wait_ge(sT_ps, i + (base + 1))
                act.activation(sTh[:, :], bankM[:, 0, :], ACT.Copy).then_inc(sTh_s, 1)
                for k in range(HT):
                    act.wait_ge(h_ps, i * HT + (base * HT + k + 1))
                    act.activation(hT[:, k, :], h_bank(k), ACT.Gelu).then_inc(gelu_s, 1)

            def combine_weights(base, i, nxt):
                act.wait_ge(nrmax_s, i + (base + 2))
                for t in range(TT):
                    act.activation(E_c[:, t, :], bankL[:, t, :], ACT.Exp, bias=nrowmax[:, t:t + 1],
                                   accum_out=rowsum[:, nxt, t:t + 1]).then_inc(Ec_s, 1)

            def parts(base, i, nxt, has):
                if has(0):
                    act.wait_ge(proc_ps, i + (base + 1))
                    act.activation(proch[:, :, :].rearrange("p s d -> p (s d)"), bankH[:, 1, :], ACT.Copy)\
                       .then_inc(proch_s, 1)
                if has(1):
                    act.wait_ge(Ld_ps, i + (base + 2))
                    act.activation(E_dh[:, :, :], bankL[:, :, :], ACT.Exp).then_inc(Edh_s, 1)
                    for t in range(TT):
                        act.activation(E_d[:, t, :], bankL[:, t, :], ACT.Exp).then_inc(Ed_s, 1)

            def transposed_weights(base, i, nxt):
                act.wait_ge(EcT_ps, i + (base + 2))
                act.activation(E_cTh[:, nxt, :, :], LT, ACT.Copy, scale=HALF).then_inc(EcTh_s, 1)

            def body1(i, par, has):
                if has(0):
                    second_half(0, i)
                if has(1):
                    combine_weights(0, i, 1 - par)
                if has(-2):
                    act.wait_ge(mT_ps, i - 1)
                    act.activation(mT[:, :], bankH[:, 0, :], ACT.Copy).then_inc(mT_s, 1)
                parts(0, i, 1 - par, has)
                if has(-2):
                    uz = bankM[:, 0, :].rearrange("p (h r c) -> p h r c", h=2, r=2)
                    act.wait_ge(uz_ps, i - 1)
                    act.activation(u_part(0, i - 2), uz[:, :, 0, :], ACT.Copy).then_inc(uh_s, 1)
                    if has(-3):
                        act.wait_ge(e1_s, i - 2)
                    act.activation(sig[:, :, :], uz[:, :, 1, :], ACT.Exp, scale=-1.0).then_inc(e_s, 1)
                    act.activation(z[:, :, bass.ds(i - 2, 1), :].rearrange("p h o c -> p h (o c)"), uz[:, :, 1, :],
                                   ACT.Copy).then_inc(zc_s, 1)
                if has(1):
                    transposed_weights(0, i, 1 - par)

            def body2(i, par, has):
                if has(0):
                    second_half(NB, i)
                if has(1):
                    combine_weights(NB, i, 1 - par)
                if has(4):
                    act.wait_ge(ygT_ps, i + 5)
                    act.activation(mT[:, 0:SEQ], bankH[:, 0, 0:SEQ], ACT.Copy).then_inc(ygT_s, 1)
                parts(NB, i, 1 - par, has)
                if has(1):
                    transposed_weights(NB, i, 1 - par)

            steps(act, body1, **FFN1)

            act.sem_inc(y_s, RING)

            def take_y(c, s):
                act.wait_ge(conv_ps, c + 1)
                act.activation(y_of(c * CH, CH), conv_bank(s), ACT.Copy).then_inc(y_s, 1)
            conv_chunks(take_y)
            steps(act, body2, **FFN2)

        @block.vector
        def _(dve):
            count = [0]

            def link(ins):
                count[0] += 1
                ins.then_inc(dve_seq, 1)
                dve.wait_ge(dve_seq, count[0])

            for h in range(2):
                e = dve.memset(xnh[:, h, :, D:D + 1], 1.0)
            dve.memset(ones[:, :], 1.0).then_inc(ones_s, 1)
            link(dve.memset(brep[:, 0:P], 0.0))
            link(dve.memset(brep[0:1, 0:P], 1.0))
            link(dve.memset(brep[64:65, 0:P], 1.0))
            dve.tensor_copy(oneh[:, :], brep[:, 0:P]).then_inc(ones_s, 1)
            dve.wait_ge(w_g, 32)
            dve.wait_ge(w_se, 16)
            link(dve.tensor_tensor(gslot[:, :], gslot[:, :], gxrow[:, :], ALU.mult))
            dve.tensor_tensor(se_n[:, :, :], raw_se[:, :, :],
                              gslot[:, :].unsqueeze(1).to_broadcast([P, ST, D]), ALU.mult).then_inc(se_row, 1)
            dve.wait_ge(se_sum, 1)
            dve.tensor_scalar(ms[:, :], ss[:, :], 1.0 / D, RMS_EPS * RMS_EPS / D, ALU.mult, ALU.max).then_inc(se_floor, 1)

            def slots_scale():
                dve.wait_ge(se_row, 1)
                dve.wait_ge(se_scale, 1)
                for s in range(ST):
                    e = dve.tensor_scalar(se_n[:, s, :], se_n[:, s, :], sef[:, s:s + 1], None, ALU.mult)
                e.then_inc(se_row, 1)

            def slots_parts():
                dve.wait_ge(seT_ps, 1)
                link(dve.tensor_copy(seh[:, :], bankH[:, 0, :]))
                dve.tensor_tensor(sel[:, :], bankH[:, 0, :], seh[:, :].bitcast(F32), ALU.subtract).then_inc(se_s, 1)

            def w1_parts():
                dve.wait_ge(w_w1, 32)
                dve.wait_ge(w1h_s, 1)
                link(dve.tensor_scalar(w1g[:, :], raw_w1[:, :], gxcol[:, 0:1], None, ALU.mult))
                dve.tensor_tensor(w1l[:, :], w1g[:, :], w1h[:, :].bitcast(F32), ALU.subtract).then_inc(w1_s, 1)

            def in_rows():
                dve.wait_ge(w_io, 112)
                link(dve.tensor_tensor(inw[:, :, :], raw_in[:, :, :],
                                       brow[:, :].unsqueeze(1).to_broadcast([P, 2, D]), ALU.mult))
                link(dve.reduce_sum(bias[:, :], inw[:, :, :], AX))
                link(dve.tensor_tensor(bias[:, :], bias[:, :], inb[:, :], ALU.add))
                link(dve.tensor_tensor(inw[:, :, :], raw_in[:, :, :],
                                       grow[:, :].unsqueeze(1).to_broadcast([P, 2, D]), ALU.mult))
                link(dve.tensor_tensor(insq[:, 0, :], inw[:, 0, :], inw[:, 0, :], ALU.mult))
                link(dve.reduce_sum(n2[:, :], insq[:, 0, :], AX))
                dve.tensor_scalar(n2[:, :], n2[:, :], float(D) * 1.01, 1e-30, ALU.mult, ALU.max).then_inc(n2_s, 1)

            def in_scale():
                dve.wait_ge(n2_s, 1)
                dve.wait_ge(nrm_s, 1)
                link(dve.tensor_scalar(nbias[:, :], bias[:, 0:1], -1.0, None, ALU.mult))
                link(dve.tensor_tensor(nbias[:, :], bias[:, 0:1], nbias[:, :], ALU.max))
                link(dve.scalar_tensor_tensor(out=ubound[:, :], in0=n2[:, :], scalar=nrm[:, 0:1], in1=nbias[:, :],
                                              op0=ALU.mult, op1=ALU.add))
                link(dve.tensor_scalar(ubound[:, :], ubound[:, :], 1.0 / HALF, None, ALU.mult))
                link(dve.reciprocal(rub[:, :], ubound[:, :]))
                link(dve.tensor_scalar(inw[:, 0, :], inw[:, 0, :], rub[:, 0:1], None, ALU.mult))
                link(dve.tensor_scalar(bias[:, 0:1], bias[:, 0:1], rub[:, 0:1], None, ALU.mult))
                dve.wait_ge(cbs_s, 1)
                dve.tensor_scalar(oscale[:, :], ubound[:, :], cbs[:, 0:1], None, ALU.mult).then_inc(in_row, 1)

            def in_parts():
                dve.wait_ge(inT_ps, 1)
                link(dve.tensor_copy(brep[:, :], bankH[:, 0, 0:2 * D]))
                dve.tensor_copy(inT[:, :], bankM[:, 0, 0:2 * D])
                dve.tensor_scalar(outT[:, :], bankM[:, 0, 2 * D:3 * D], oscale[:, 0:1], None, ALU.mult)\
                   .then_inc(bias_s, 1)

            def bias_parts():
                link(dve.tensor_copy(binh[:, :], brep[:, :]))
                link(dve.tensor_tensor(brep[:, :], brep[:, :], binh[:, :].bitcast(F32), ALU.subtract))
                dve.tensor_copy(binh[64:P, :], brep[64:P, :]).then_inc(mix_set, 1)

            def proc_bound():
                dve.wait_ge(bound_ps, 1)
                link(dve.reduce_max(w2max[:, :], bankH[:, 1, 0:D], AX))
                link(dve.tensor_tensor(b2[:, :], w2max[:, :], bankH[:, 1, D:D + 1], ALU.mult))
                dve.tensor_scalar(b2[:, :], b2[:, :], D * 1.01 / (WIDE * WIDE), 1e-30, ALU.mult, ALU.max)\
                   .then_inc(b2_s, 1)

            def w2_scale():
                dve.wait_ge(rb_s, 1)
                dve.wait_ge(w_w2, 16)
                dve.tensor_scalar(w2s[:, :, :], raw_w2[:, :, :], rb[:, 0:1], None, ALU.mult).then_inc(w2_s, 1)
                link(dve.reciprocal(bscale[:, :], rb[:, :]))
                link(dve.tensor_scalar(cscale[:, :], bscale[:, :], 0.5 / HALF, None, ALU.mult))

            def silu_z(i):
                z_b = z[:, :, bass.ds(i - 3, 1), :].rearrange("p h o c -> p h (o c)")
                dve.wait_ge(e_s, i - 2)
                dve.tensor_scalar(upd[:, :, :], sig[:, :, :], 1.0, None, ALU.add).then_inc(e1_s, 1)
                dve.wait_ge(e1_s, i - 2)
                dve.reciprocal(rsig[:, :, :], upd[:, :, :]).then_inc(sig_s, 1)
                dve.wait_ge(sig_s, i - 2)
                dve.wait_ge(zc_s, i - 2)
                dve.tensor_tensor(z_b, z_b, rsig[:, :, :], ALU.mult).then_inc(z_s, 1)

            def ffn_body(base, i, par, has):
                first = base == 0
                nxt = 1 - par
                if has(1):
                    if first and has(-1):
                        dve.wait_ge(x_s, i)
                    if not first and has(3):
                        dve.wait_ge(mixed, i + 4)
                    dve.wait_ge(L_ps, i + (base + 2))
                    dve.reduce_max(rowmax[:, :], bankL[:, :, :], AX).then_inc(rmax_s, 1)
                    dve.wait_ge(LT_ps, i + (base + 2))
                    dve.reduce_max(colmax[:, :], LT, AX).then_inc(cmax_s, 1)
                    dve.wait_ge(rmax_s, i + (base + 2))
                    dve.tensor_scalar(nrowmax[:, :], rowmax[:, :], -1.0, None, ALU.mult).then_inc(nrmax_s, 1)
                    dve.wait_ge(cmax_s, i + (base + 2))
                    for k, slack in enumerate((ROUND, -ROUND)):
                        e = dve.tensor_scalar(ncm[:, k, :], colmax[:, :], -1.0 - slack, SHIFT, ALU.mult, ALU.add)
                    e.then_inc(ncm_s, 1)
                    dve.wait_ge(ncm_s, i + (base + 2))
                    dve.tensor_tensor(ncolmax[:, :], ncm[:, 0, :], ncm[:, 1, :], ALU.min).then_inc(ncmax_s, 1)
                elif first and has(-1):
                    dve.wait_ge(x_s, i)
                elif not first and has(3):
                    dve.wait_ge(mixed, i + 4)
                if first and i_is(i, -2):
                    slots_scale()
                if has(2):
                    dve.wait_ge(xT_ps, i + (base + 3))
                    dve.tensor_copy(xTh[:, par, :], bankM[:, 1, 0:SEQ]).then_inc(xTh_s, 1)
                    dve.wait_ge(xTh_s, i + (base + 3))
                    dve.tensor_tensor(xTl[:, par, :], bankM[:, 1, 0:SEQ], xTh[:, par, :].bitcast(F32),
                                      ALU.subtract).then_inc(xT_s, 1)
                if first and i_is(i, -2):
                    slots_parts()
                if first and i_is(i, -1):
                    proc_bound()
                    w1_parts()
                if has(3):
                    if first and type(i) is int and (i + 3) % XB == 0:
                        dve.wait_ge(x_in_s[(i + 3) // XB], 16)
                    if first and i_is(i, 2):
                        for c in range((i + 3) // XB + 1, XCH):
                            dve.wait_ge(x_in_s[c], 16)
                    for t in range(TT):
                        e = dve.bn_stats(bn6[:, t, :], tile((i + 3) * TT + t).rearrange("p o d -> p (o d)"))
                    e.then_inc(bn_s, 1)
                again = first and has(-1)
                if again:
                    for t in range(TT):
                        e = dve.bn_stats(bnm[:, t, :], tile((i - 1) * TT + t).rearrange("p o d -> p (o d)"))
                    e.then_inc(mbn_s, 1)
                if first and i_is(i, 0):
                    in_rows()
                if first and i_is(i, 1):
                    in_scale()
                if first and i_is(i, 2):
                    bias_parts()
                draining = type(i) is int and i >= NB
                if first and has(-3) and not draining:
                    silu_z(i)
                if has(3):
                    dve.wait_ge(bn_s, i + (base + 4))
                if again:
                    dve.wait_ge(mbn_s, i)
                if has(0):
                    dve.wait_ge(proch_s, i + (base + 1))
                    dve.tensor_tensor(procl[:, :, :].rearrange("p s d -> p (s d)"), bankH[:, 1, :],
                                      proch[:, :, :].rearrange("p s d -> p (s d)"), ALU.subtract).then_inc(proc_s, 1)
                if has(3):
                    for t in range(TT):
                        e = dve.bn_aggr(mean_var[:, nxt, t, :], bn6[:, t, :])
                    e.then_inc(mv_s, 1)
                if again:
                    for t in range(TT):
                        e = dve.bn_aggr(new_mv[:, t, :], bnm[:, t, :])
                    e.then_inc(mag_s, 1)
                if has(3):
                    dve.wait_ge(mv_s, i + (base + 4))
                    dve.tensor_scalar(floor_var[:, nxt, :], mean_var[:, nxt, :, 1],
                                      LN_EPS * RMS_EPS * RMS_EPS / D, None, ALU.max).then_inc(var_s, 1)
                if again:
                    dve.wait_ge(mag_s, i)
                    dve.tensor_scalar(mix_var[:, 0, nxt, :], new_mv[:, :, 1], 1.0 + LN_EPS, LN_EPS * LN_EPS,
                                      ALU.mult, ALU.add)
                    dve.tensor_scalar(mix_var[:, 1, nxt, :], new_mv[:, :, 1], LN_EPS, None, ALU.add).then_inc(mvar_s, 1)
                    dve.tensor_scalar(nmean[:, bass.ds((i - 1) * TT, TT)], new_mv[:, :, 0], -1.0, None, ALU.mult)\
                       .then_inc(mvar_s, 1)
                if first and i_is(i, 1):
                    in_parts()
                if first and has(-3) and draining:
                    silu_z(i)
                side = not first and has(4)
                if has(1):
                    for t in range(TT):
                        dve.wait_ge(Ed_s, i * TT + ((base + 1) * TT + 1 + t))
                        dve.tensor_tensor(E_dl[:, t, :], E_d[:, t, :], E_dh[:, t, :], ALU.subtract).then_inc(Edl_s, 1)
                if first and has(-2):
                    uz = bankM[:, 0, :].rearrange("p (h r c) -> p h r c", h=2, r=2)
                    dve.wait_ge(uh_s, i - 1)
                    dve.wait_ge(zc_s, i - 1)
                    dve.tensor_tensor(u_part(1, i - 2), uz[:, :, 0, :], u_part(0, i - 2), ALU.subtract).then_inc(u_s, 1)
                if side:
                    dve.wait_ge(resb_s, i + 5)
                    dve.wait_ge(o_ps, i + 5)
                    dve.tensor_tensor(upd[:, :, :], bankM[:, 0, 0:SEQ].rearrange("p (h d) -> p h d", h=2),
                                      resb[:, :, :], ALU.add).then_inc(upd_s, 1)
                if has(1):
                    dve.wait_ge(slots_ps, i + (base + 2))
                    dve.reciprocal(rslot[:, :, :], slot_ps[:, :, :, D]).then_inc(rslot_s, 1)
                    dve.wait_ge(Ec_s, i * TT + (base + 2) * TT)
                    dve.reciprocal(rrow[:, :], rowsum[:, nxt, :]).then_inc(rrow_s, 1)
                    dve.wait_ge(rslot_s, i + (base + 2))
                    for a in range(2):
                        dve.tensor_tensor(slots_n[:, 2 * a:2 * a + 2, :], slot_ps[:, a, :, 0:D],
                                          rslot[:, a, :].unsqueeze(2).to_broadcast([P, 2, D]), ALU.mult)\
                           .then_inc(slots_s, 1)
                if has(1):
                    dve.wait_ge(EcTh_s, i + (base + 2))
                    dve.scalar_tensor_tensor(out=E_cTl[:, nxt, :, :], in0=LT, scalar=HALF, in1=E_cTh[:, nxt, :, :],
                                             op0=ALU.mult, op1=ALU.subtract).then_inc(EcT_s, 1)
                    dve.wait_ge(sTh_s, i + (base + 2))
                    dve.tensor_tensor(sTl[:, :], bankM[:, 0, :], sTh[:, :].bitcast(F32), ALU.subtract).then_inc(sT_s, 1)
                if side:
                    dve.wait_ge(upd_s, i + 5)
                    dve.tensor_scalar(updc[:, :, :], upd[:, :, :], CLIP, -CLIP, ALU.min, ALU.max).then_inc(updc_s, 1)
                if first and i_is(i, -1):
                    w2_scale()
                if has(1):
                    dve.wait_ge(rrow_s, i + (base + 2))
                    dve.tensor_scalar(hrrow[:, nxt, :], rrow[:, :], cscale[:, 0:1], None, ALU.mult).then_inc(hrrow_s, 1)
                if side:
                    dve.wait_ge(updc_s, i + 5)
                    dve.tensor_tensor(tile((i + 4) * TT, TT), tile((i + 4) * TT, TT), updc[:, :, :], ALU.add)\
                       .then_inc(mixed, 1)
                if has(3):
                    dve.wait_ge(scale_s, i + (base + 4))
                    for t in range(TT):
                        e = dve.tensor_scalar(xn[:, nxt, t, 0:D].unsqueeze(1), tile((i + 3) * TT + t),
                                              mean_var[:, nxt, t, 0:1], scale_x[:, nxt, t:t + 1],
                                              ALU.subtract, ALU.mult)
                    e.then_inc(xn_s, 1)
                if has(0):
                    dve.wait_ge(hrrow_s, i + (base + 1))
                    dve.wait_ge(out_ps, i + (base + 1))
                    for t in range(TT):
                        n = i * TT + t
                        e = dve.scalar_tensor_tensor(out=tile(n), in0=bankM[:, 1, t * D:(t + 1) * D].unsqueeze(1),
                                                     scalar=hrrow[:, par, t:t + 1], in1=tile(n),
                                                     op0=ALU.mult, op1=ALU.add)
                    e.then_inc(x_s, 1)
            steps(dve, lambda i, par, has: ffn_body(0, i, par, has), **FFN1)
            steps(dve, lambda i, par, has: ffn_body(NB, i, par, has), **FFN2)

        @block.tensor
        def _(pe):
            def combine(par, t):
                dst = bankM[:, 1, t * D:(t + 1) * D]
                for s in range(ST):
                    eh, el = (m[:, par, s, t * P:(t + 1) * P] for m in (E_cTh, E_cTl))
                    pe.matmul(dst, eh, proch[:, s, :], start=(s == 0), stop=False)
                    pe.matmul(dst, eh, procl[:, s, :], start=False, stop=False)
                    e = pe.matmul(dst, el, proch[:, s, :], start=False, stop=(s == ST - 1))
                return e

            def set_up_slots():
                pe.wait_ge(se_row, 2)
                for s in range(ST):
                    e = pe.transpose(bankH[:, 0, s * P:(s + 1) * P], se_n[:, s, :], ident[:, :])
                e.then_inc(seT_ps, 1)
                pe.wait_ge(ones_s, 1)
                pe.wait_ge(wsum_s, 2)
                for k in range(HT):
                    pe.matmul(bankH[:, 1, 0:D], ones[:, :], w2sq[:, k, :], start=(k == 0), stop=(k == HT - 1))
                pe.matmul(bankH[:, 1, D:D + 1], ones[:, :], w1sum[:, :], start=True, stop=True).then_inc(bound_ps, 1)

            def set_up_mixer():
                pe.wait_ge(in_row, 1)
                pe.wait_ge(w_io, 112)
                for r in range(2):
                    pe.transpose(bankM[:, 0, r * D:(r + 1) * D], inw[:, r, :], ident[:, :])
                    pe.matmul(bankH[:, 0, r * D:(r + 1) * D], bias[:, r:r + 1].to_broadcast([P, P]), ident[:, :],
                              start=True, stop=True)
                pe.transpose(bankM[:, 0, 2 * D:3 * D], raw_out[:, :], ident[:, :]).then_inc(inT_ps, 1)

            def ffn_body(base, i, par, has):
                first = base == 0
                nxt = 1 - par
                side = has(-2) if first else has(4)
                n_side = i - 1 if first else i + 5
                if has(1):
                    pe.wait_ge(xT_s, i + (base + 2))
                    if first and i_is(i, -1):
                        pe.wait_ge(se_s, 1)
                    pe.matmul(bankL[:, 0, :], xTh[:, nxt, 0:P], seh[:, :], start=True, stop=False)
                if has(0):
                    if first and has(-3):
                        pe.wait_ge(u_s, i - 2)
                    if not first:
                        pe.wait_ge(upd_s, min(i + 4, NB) if type(i) is int else i + 4)
                    for s in range(ST):
                        if s % 2 == 0:
                            pe.wait_ge(slots_s, i * 2 + (base * 2 + 1 + s // 2))
                        e = pe.transpose(bankM[:, 0, s * P:(s + 1) * P], slots_n[:, s, :], ident[:, :])
                    e.then_inc(sT_ps, 1)
                if has(1):
                    pe.matmul(bankL[:, 0, :], xTh[:, nxt, 0:P], sel[:, :], start=False, stop=False)
                    pe.matmul(bankL[:, 0, :], xTl[:, nxt, 0:P], seh[:, :], start=False, stop=True)
                    split3(pe, bankL[:, 1, :], xTh[:, nxt, P:SEQ], xTl[:, nxt, P:SEQ], seh[:, :], sel[:, :])\
                        .then_inc(L_ps, 1)
                if has(1):
                    if has(0):
                        pe.wait_ge(EcT_s, i + (base + 1))
                    for s in range(ST):
                        e = pe.matmul(LT[:, s, :], seh[:, s * P:(s + 1) * P], xTh[:, nxt, :], start=True, stop=True)
                    e.then_inc(LT_ps, 1)
                if has(0):
                    pe.wait_ge(sT_s, i + (base + 1))
                    if first and i_is(i, 0):
                        pe.wait_ge(w1_s, 1)
                        pe.wait_ge(w2_s, 1)
                    for k in range(HT):
                        if k == 3:
                            pe.wait_ge(gelu_s, i * HT + (base * HT + 1))
                        split3(pe, h_bank(k), w1h[:, k * P:(k + 1) * P], w1l[:, k * P:(k + 1) * P],
                               sTh[:, :], sTl[:, :]).then_inc(h_ps, 1)
                if has(2):
                    pe.wait_ge(xn_s, i + (base + 3))
                    if has(-1):
                        pe.wait_ge(x_s, i + base)
                    if has(1):
                        pe.wait_ge(xT_s, i + (base + 2))
                    for t in range(TT):
                        e = pe.transpose(bankM[:, 1, t * P:(t + 1) * P], xn[:, par, t, :], ident[:, :])
                    e.then_inc(xT_ps, 1)
                if first and i_is(i, -2):
                    set_up_slots()
                if has(0):
                    for k in range(2):
                        pe.wait_ge(gelu_s, i * HT + (base * HT + 2 + k))
                        project(k)
                if side:
                    if has(0):
                        pe.wait_ge(gelu_s, i * HT + (base * HT + HT))
                    if first:
                        pe.wait_ge(xm_s, n_side)
                        for t in range(TT):
                            pe.transpose(bankH[:, 0, t * P:(t + 1) * P], xm[:, t, :], ident[:, :])
                            e = pe.transpose(bankH[:, 0, SEQ + t * P:SEQ + (t + 1) * P], xm[:, t, :], flip[:, :])
                        e.then_inc(mT_ps, 1)
                    else:
                        pe.wait_ge(yg_s, n_side)
                        for t in range(TT):
                            e = pe.transpose(bankH[:, 0, t * P:(t + 1) * P], yg[:, t, :], ident[:, :])
                        e.then_inc(ygT_ps, 1)
                if has(0):
                    pe.wait_ge(gelu_s, i * HT + (base * HT + HT))
                    project(2)
                    project(3).then_inc(proc_ps, 1)
                if has(1):
                    pe.wait_ge(Ec_s, i * TT + ((base + 2) * TT))
                    pe.wait_ge(ncmax_s, i + (base + 2))
                    for t in range(TT):
                        for s in range(ST):
                            e = pe.matmul(bankL[:, t, s * P:(s + 1) * P], ncolmax[:, s:s + 1].to_broadcast([P, P]),
                                          identb[:, :], start=False, stop=True, skip_group_check=True)
                    e.then_inc(Ld_ps, 1)
                    for s in range(ST):
                        for t in range(TT):
                            e = pe.transpose(LT[:, s, t * P:(t + 1) * P], E_c[:, t, s * P:(s + 1) * P], ident[:, :])
                    e.then_inc(EcT_ps, 1)
                if first and i_is(i, 1):
                    set_up_mixer()
                if side and first:
                    pe.wait_ge(mT_s, n_side)
                    if i_is(i, 2):
                        pe.wait_ge(mix_set, 1)
                        pe.wait_ge(ones_s, 2)
                    if not has(0):
                        pe.wait_ge(u_s, i - 2)
                    for t in range(TT):
                        dst = bankM[:, 0, t * 2 * D:(t + 1) * 2 * D]
                        pe.matmul(dst, oneh[:, :], binh[:, :], start=True, stop=False, skip_group_check=True)
                        pe.matmul(dst[:, 0:D], mT[:, SEQ + t * P:SEQ + (t + 1) * P], inT[:, 0:D],
                                  start=False, stop=True, skip_group_check=True)
                        e = pe.matmul(dst[:, D:2 * D], mT[:, t * P:(t + 1) * P], inT[:, D:2 * D],
                                      start=False, stop=True, skip_group_check=True)
                    e.then_inc(uz_ps, 1)
                if side and not first:
                    pe.wait_ge(ygT_s, n_side)
                    if not has(0) and has(3):
                        pe.wait_ge(upd_s, i + 4)
                    for t in range(TT):
                        e = pe.matmul(bankM[:, 0, t * D:(t + 1) * D], mT[:, t * P:(t + 1) * P], outT[:, :],
                                      start=True, stop=True)
                    e.then_inc(o_ps, 1)
                def slots_passes(parts, first_pass, last_pass):
                    for s in range(ST):
                        dst = slot_ps[:, s // 2, s % 2, :]
                        for n, (ed, xp, cols) in enumerate(parts):
                            for t in range(TT):
                                e = pe.matmul(dst[:, 0:cols], ed[:, t, s * P:(s + 1) * P], xp[:, nxt, t, :],
                                              start=(first_pass and s % 2 == 0 and n == 0 and t == 0),
                                              stop=(last_pass and t == TT - 1), skip_group_check=True)
                    return e

                if has(1):
                    pe.wait_ge(Edh_s, i + (base + 2))
                    pe.wait_ge(xnp_s, i + (base + 2))
                    if has(0):
                        pe.wait_ge(proc_s, i + (base + 1))
                    if first and i_is(i, -1):
                        pe.wait_ge(b2_s, 1)
                    if first and i_is(i, 1):
                        pe.wait_ge(bias_s, 1)
                    if side:
                        pe.wait_ge(mT_s if first else ygT_s, n_side)
                    slots_passes(((E_dh, xnh, D + 1), (E_dh, xnl, D)), True, False)
                if has(0):
                    pe.wait_ge(proc_s, i + (base + 1))
                    if has(2):
                        pe.wait_ge(xT_s, i + (base + 3))
                    combine(par, 0)
                if has(1):
                    pe.wait_ge(Edl_s, i * TT + ((base + 2) * TT))
                    slots_passes(((E_dl, xnh, D + 1),), False, True).then_inc(slots_ps, 1)
                if has(0):
                    combine(par, 1).then_inc(out_ps, 1)

            def project(k):
                for s in range(ST):
                    e = pe.matmul(bankH[:, 1, s * D:(s + 1) * D], hT[:, k, s * P:(s + 1) * P], w2s[:, k, :],
                                  start=(k == 0 and s == 0), stop=(k == HT - 1), skip_group_check=True)
                return e

            pe.wait_ge(consts, 10)
            steps(pe, lambda i, par, has: ffn_body(0, i, par, has), **FFN1)

            pe.wait_ge(u_s, NB)
            pe.wait_ge(x_s, NB)

            def convolve(g, s):
                pe.wait_ge(toep_s[s], g // RING * 32 + 32)
                pe.wait_ge(y_s, g + 1)
                for c in range(CH):
                    dst = conv_bank(s)[:, c, :]
                    uc = u[:, bass.ds(g * CH + c, 1), :, :]
                    uh = uc[:, :, 0, :].rearrange("p o n -> p (o n)")
                    ul = uc[:, :, 1, :].rearrange("p o n -> p (o n)")
                    near = [toeplitz(s, c, part, 0) for part in range(2)]
                    far = [toeplitz(s, c, part, P) for part in range(2)]
                    pe.matmul(dst, near[0], uh, start=True, stop=False, skip_group_check=True)
                    pe.matmul(dst, near[0], ul, start=False, stop=False, skip_group_check=True)
                    pe.matmul(dst, near[1], uh, start=False, stop=False, skip_group_check=True)
                    pe.matmul(dst[:, NB:], far[0], uh[:, 0:NB], start=False, stop=False, skip_group_check=True)
                    pe.matmul(dst[:, NB:], far[0], ul[:, 0:NB], start=False, stop=False, skip_group_check=True)
                    e = pe.matmul(dst[:, NB:], far[1], uh[:, 0:NB], start=False, stop=True, skip_group_check=True)
                e.then_inc(conv_ps, 1)
            conv_chunks(convolve)
            steps(pe, lambda i, par, has: ffn_body(NB, i, par, has), **FFN2)


_INS = ['L0_attn_x', 'L0_attn_A_log', 'L0_attn_B_param', 'L0_attn_C_param', 'L0_attn_log_dt', 'L0_attn_in_w',
        'L0_attn_in_b', 'L0_attn_out_w', 'L0_attn_out_b', 'L0_attn_ln_g', 'L0_attn_ln_b', 'L0_ffn_gamma_x',
        'L0_ffn_gamma_slot', 'L0_ffn_slot_embeds', 'L0_ffn_w1', 'L0_ffn_w2']


def kernel(**inputs):
    import numpy as _np
    import concourse.bacc as _bacc
    from concourse import mybir as _mybir
    from concourse.bass_utils import run_bass_kernel_spmd as _run

    nc = _bacc.Bacc("TRN2", target_bir_lowering=False, num_devices=1)
    arrays, args = {}, []
    for name in _INS:
        a = _np.ascontiguousarray(inputs[name])
        arrays[f"in_{name}"] = a
        args.append(nc.dram_tensor(f"in_{name}", a.shape, _mybir.dt.from_np(a.dtype), kind="ExternalInput").ap())
    args.append(nc.dram_tensor("out_x", inputs['L0_attn_x'].shape, _mybir.dt.from_np(_np.dtype("float32")),
                               kind="ExternalOutput").ap())
    macaron_kernel(nc, *args)
    return _run(nc, [arrays], core_ids=[0]).results[0]["out_x"]
```

```python
import math
from contextlib import ExitStack

import concourse.bass as bass
from concourse import mybir

F32 = mybir.dt.float32
F32R = mybir.dt.float32r
F16 = mybir.dt.float16
BF16 = mybir.dt.bfloat16
ALU = mybir.AluOpType
ACT = mybir.ActivationFunctionType
AX = mybir.AxisListType.X

P = 128
LN_EPS = 1e-5
RMS_EPS = 1e-12
LOG_A_MIN = math.log(1e-8)
DT_MIN, DT_MAX = 1e-4, 1.0
CLIP = 10.0
HALF = 4096.0
WIDE = 32768.0
SHIFT = math.log(HALF)
ROUND = 2.0 ** -8


def macaron_kernel(nc, x_in, A_log, B_param, C_param, log_dt, in_w, in_b, out_w, out_b,
                   ln_g, ln_b, gamma_x, gamma_slot, slot_embeds, w1, w2, out):
    NB, SEQ, D = x_in.shape
    TT = SEQ // P
    NT = NB * TT
    NS = A_log.shape[1]
    SLOTS = slot_embeds.shape[0] * slot_embeds.shape[1]
    ST = SLOTS // P
    HID = w1.shape[1]
    HT = HID // P
    assert D == P and TT == 2 and ST == 4 and HT == 4 and NB % 2 == 0

    CH = 8
    NCH = D // CH
    RING = 10
    EARLY = 5
    BANKS = 8
    LAG0 = SEQ // 2 - 1
    KP = 384
    XCH = 8
    XB = NB // XCH

    x_dram = x_in.rearrange("b (h p) d -> p (b h) d", p=P)
    out_dram = out.rearrange("b (h p) d -> p (b h) d", p=P)
    resp_dram = nc.dram_tensor("resp_dram", [D, 2, KP], F16, kind="Internal")

    ctx = ExitStack()
    with ctx:
        def sb(name, shape, dt=F32, where=ctx):
            return where.enter_context(nc.sbuf_tensor(name, shape, dt))

        def psum(name, shape):
            return ctx.enter_context(nc.psum_tensor(name, shape, F32))

        def sem(name):
            return ctx.enter_context(nc.semaphore(name))

        x = sb("x", [P, NT, D])
        ident = sb("ident", [P, P])
        identb = sb("identb", [P, P], BF16)
        flip = sb("flip", [P, P])
        w1h = sb("w1h", [P, HID], F32R)
        w1l = sb("w1l", [P, HID], F32R)
        w2s = sb("w2s", [P, HT, D])
        seh = sb("seh", [P, SLOTS], F32R)
        sel = sb("sel", [P, SLOTS], F32R)
        inT = sb("inT", [P, 2 * D])
        binh = sb("binh", [P, 2 * D], F32R)
        oneh = sb("oneh", [P, P], F32R)
        outT = sb("outT", [P, D])
        obias = sb("obias", [P, D])
        respp = sb("respp", [P, 2, KP], F16)
        mean_var = sb("mean_var", [P, 2, TT, 2])
        floor_var = sb("floor_var", [P, 2, TT])
        scale_x = sb("scale_x", [P, 2, TT])
        new_mv = sb("new_mv", [P, TT, 2])
        mix_var = sb("mix_var", [P, 2, 2, TT])
        mix_scale = sb("mix_scale", [P, 2, TT])
        res2 = sb("res2", [P, TT, D])
        nmean = sb("nmean", [P, NT])
        rstd = sb("rstd", [P, NT])
        mhalf = sb("mhalf", [P, ST])
        bn6 = sb("bn6", [P, 2, 6])
        bnm = sb("bnm", [P, 2, 6])
        u = sb("u", [P, D, 2, 2 * NB], F16)
        z = sb("z", [P, 2, NB, D])
        xm = sb("xm", [P, TT, D])
        xc = sb("xc", [P, TT, D])
        mT = sb("mT", [P, 2 * SEQ])
        upd = sb("upd", [P, TT, D])
        sig = sb("sig", [P, TT, D])
        rsig = sb("rsig", [P, TT, D])

        xn = sb("xn", [P, 2, TT, D], F32)
        xnh = sb("xnh", [P, 2, TT, D + 1], F16)
        xnl = sb("xnl", [P, 2, TT, D], F16)
        zero = sb("zero", [P, TT])
        cscale = sb("cscale", [P, 1])
        colmax = sb("colmax", [P, ST], F32)
        ncolmax = sb("ncolmax", [P, ST], BF16)
        ncm = sb("ncm", [P, 2, ST], F32)
        rowmax = sb("rowmax", [P, TT], F32)
        nrowmax = sb("nrowmax", [P, TT], F32)
        rowsum = sb("rowsum", [P, 2, TT], F32)
        rrow = sb("rrow", [P, TT], F32)
        hrrow = sb("hrrow", [P, 2, TT], F32)
        rslot = sb("rslot", [P, 2, 2], F32)
        ffn = ExitStack()
        E_d = sb("E_d", [P, TT, SLOTS], F32, ffn)
        E_dh = sb("E_dh", [P, TT, SLOTS], F16, ffn)
        E_dl = sb("E_dl", [P, TT, SLOTS], F16, ffn)
        hT = sb("hT", [P, HT, SLOTS], F32, ffn)
        E_cTh = sb("E_cTh", [P, 2, ST, SEQ], F16, ffn)
        E_cTl = sb("E_cTl", [P, 2, ST, SEQ], F16, ffn)
        E_c = sb("E_c", [P, TT, SLOTS], F32, ffn)
        sTh = sb("sTh", [P, SLOTS], F32R, ffn)
        sTl = sb("sTl", [P, SLOTS], F32R, ffn)
        slots_n = sb("slots_n", [P, ST, D], F32, ffn)
        xTh = sb("xTh", [P, 2, SEQ], F32R, ffn)
        xTl = sb("xTl", [P, 2, SEQ], F32R, ffn)
        proch = sb("proch", [P, ST, D], F16, ffn)
        procl = sb("procl", [P, ST, D], F16, ffn)
        ffn.close()
        toep_late = sb("toep_late", [P, RING - EARLY, CH, 2, SEQ], F16)
        setup = ExitStack()
        raw_w1 = sb("raw_w1", [P, HID], F32, setup)
        raw_se = sb("raw_se", [P, ST, D], F32, setup)
        raw_in = sb("raw_in", [P, 2, D], F32, setup)
        raw_out = sb("raw_out", [P, D], F32, setup)
        gslot = sb("gslot", [P, D], F32, setup)
        gxrow = sb("gxrow", [P, D], F32, setup)
        grow = sb("grow", [P, D], F32, setup)
        brow = sb("brow", [P, D], F32, setup)
        gxcol = sb("gxcol", [P, 1], F32, setup)
        inb = sb("inb", [P, 2], F32, setup)
        Alog = sb("Alog", [P, NS], F32, setup)
        Bp = sb("Bp", [P, NS], F32, setup)
        Cp = sb("Cp", [P, NS], F32, setup)
        ldt = sb("ldt", [P, 1], F32, setup)
        mone = sb("mone", [P, 1], F32, setup)
        raw_w2 = sb("raw_w2", [P, HT, D], F32, setup)
        w1sq = sb("w1sq", [P, HID], F32, setup)
        w2sq = sb("w2sq", [P, HT, D], F32, setup)
        w1sum = sb("w1sum", [P, 1], F32, setup)
        ones = sb("ones", [P, P], F32, setup)
        w2max = sb("w2max", [P, 1], F32, setup)
        b2 = sb("b2", [P, 1], F32, setup)
        rb = sb("rb", [P, 1], F32, setup)
        bscale = sb("bscale", [P, 1], F32, setup)
        sq = sb("sq", [P, ST, D], F32, setup)
        ss = sb("ss", [P, ST], F32, setup)
        ms = sb("ms", [P, ST], F32, setup)
        sef = sb("sef", [P, ST], F32, setup)
        se_n = sb("se_n", [P, ST, D], F32, setup)
        w1g = sb("w1g", [P, HID], F32, setup)
        lags = sb("lags", [P, SEQ], F32, setup)
        half = sb("half", [P, NS], F32, setup)
        powers = sb("powers", [P, NS, SEQ], F32, setup)
        resp = sb("resp", [P, SEQ], F32, setup)
        expA = sb("expA", [P, NS], F32, setup)
        expdt = sb("expdt", [P, 1], F32, setup)
        dt = sb("dt", [P, 1], F32, setup)
        logA = sb("logA", [P, NS], F32, setup)
        cb = sb("cb", [P, NS], F32, setup)
        cbn = sb("cbn", [P, NS], F32, setup)
        cbs = sb("cbs", [P, 1], F32, setup)
        rcbs = sb("rcbs", [P, 1], F32, setup)
        inw = sb("inw", [P, 2, D], F32, setup)
        insq = sb("insq", [P, 2, D], F32, setup)
        bias = sb("bias", [P, 2], F32, setup)
        n2 = sb("n2", [P, 1], F32, setup)
        nrm = sb("nrm", [P, 1], F32, setup)
        ubound = sb("ubound", [P, 1], F32, setup)
        rub = sb("rub", [P, 1], F32, setup)
        nbias = sb("nbias", [P, 1], F32, setup)
        oscale = sb("oscale", [P, 1], F32, setup)
        brep = sb("brep", [P, 2 * D], F32, setup)
        setup.close()
        toep_early = sb("toep_early", [P, EARLY, CH, 2, SEQ], F16)
        res, resb, yg, updc = xc, xm, mT[:, SEQ:].rearrange("p (h d) -> p h d", h=TT), sig

        bankL = psum("bankL", [P, TT, SLOTS])
        bankT = psum("bankT", [P, 2, 512])
        bankH = psum("bankH", [P, 2, 512])
        bankM = psum("bankM", [P, 2, 512])
        LT = bankT[:, :, :].rearrange("p a (s t) -> p (a s) t", t=SEQ)
        SC = D + 2
        slot_ps = bankH[:, :, 0:2 * SC].rearrange("p a (s c) -> p a s c", c=SC)

        w_se, w_g, w_w1, w_w2, w_ssm, w_io = (sem(n) for n in ("w_se", "w_g", "w_w1", "w_w2", "w_ssm", "w_io"))
        x_in_s = [sem(f"x_in{c}") for c in range(XCH)]
        consts = sem("consts")
        dve_seq = sem("dve_seq")
        pool_seq = sem("pool_seq")
        se_sum, se_floor, se_scale, se_row = (sem(n) for n in ("se_sum", "se_floor", "se_scale", "se_row"))
        seT_ps, se_s, w1h_s, w1_s = (sem(n) for n in ("seT_ps", "se_s", "w1h_s", "w1_s"))
        wsum_s, bound_ps, b2_s, rb_s, w2_s = (sem(n) for n in ("wsum_s", "bound_ps", "b2_s", "rb_s", "w2_s"))
        ones_s, n2_s, nrm_s, in_row = (sem(n) for n in ("ones_s", "n2_s", "nrm_s", "in_row"))
        inT_ps, inT_s, bias_s, mix_set = (sem(n) for n in ("inT_ps", "inT_s", "bias_s", "mix_set"))
        ssm_exp, logA_s, powers_s, cbs_s = (sem(n) for n in ("ssm_exp", "logA_s", "powers_s", "cbs_s"))
        resp_s, resp_out = sem("resp_s"), sem("resp_out")
        toep_s = [sem(f"toep{c}") for c in range(RING)]

        bn_s, mv_s, var_s, scale_s = (sem(n) for n in ("bn_s", "mv_s", "var_s", "scale_s"))
        mbn_s, mag_s, mvar_s = (sem(n) for n in ("mbn_s", "mag_s", "mvar_s"))
        xn_s, xT_ps, xTh_s, xT_s = (sem(n) for n in ("xn_s", "xT_ps", "xTh_s", "xT_s"))
        xnh_s, xnp_s = sem("xnh_s"), sem("xnp_s")
        LT_ps, L_ps = sem("LT_ps"), sem("L_ps")
        cmax_s, ncm_s, ncmax_s, rmax_s, nrmax_s = (sem(n) for n in ("cmax_s", "ncm_s", "ncmax_s", "rmax_s", "nrmax_s"))
        EcT_ps, EcTh_s, EcT_s = (sem(n) for n in ("EcT_ps", "EcTh_s", "EcT_s"))
        Ec_s = [sem(f"Ec{t}_s") for t in range(TT)]
        Ld_ps = [sem(f"Ld{t}_ps") for t in range(TT)]
        Ed_s = [sem(f"Ed{t}_s") for t in range(TT)]
        Edh_s, Edl_s = sem("Edh_s"), sem("Edl_s")
        rrow_s, hrrow_s = sem("rrow_s"), sem("hrrow_s")
        slots_ps, rslot_s = sem("slots_ps"), sem("rslot_s")
        slots_s = [sem(f"slots{a}_s") for a in range(2)]
        sT_ps, sTh_s, sT_s = (sem(n) for n in ("sT_ps", "sTh_s", "sT_s"))
        h_ps = [sem(f"h{k}_ps") for k in range(HT)]
        gelu_s = [sem(f"gelu{k}_s") for k in range(HT)]
        proc_ps, proch_s, proc_s = (sem(n) for n in ("proc_ps", "proch_s", "proc_s"))
        out_ps, x_s = sem("out_ps"), sem("x_s")

        mscale_s, rstd_s = sem("mscale_s"), sem("rstd_s")
        xc_s, xm_s, mT_ps, mT_s = (sem(n) for n in ("xc_s", "xm_s", "mT_ps", "mT_s"))
        uz_ps, e_s, zc_s, uh_s, u_s = (sem(n) for n in ("uz_ps", "e_s", "zc_s", "uh_s", "u_s"))
        e1_s, sig_s, z_s = (sem(n) for n in ("e1_s", "sig_s", "z_s"))
        conv_ps, y_s = sem("conv_ps"), sem("y_s")
        yg_s, ygT_ps, ygT_s, o_ps = (sem(n) for n in ("yg_s", "ygT_ps", "ygT_s", "o_ps"))
        rc_s, res_s, resb_s, upd_s, updc_s, mixed = (sem(n) for n in ("rc_s", "res_s", "resb_s", "upd_s", "updc_s", "mixed"))
        stored = sem("stored")

        block = ctx.enter_context(nc.Block())

        def steps(eng, body, first, loop_from, loop_to, last):
            for i in range(first, loop_from):
                body(i, i % 2, lambda k, i=i: 0 <= i + k < NB)
            with eng.Fori(0, (loop_to - loop_from) // 2, 1) as j:
                for p in range(2):
                    body(j * 2 + (loop_from + p), (loop_from + p) % 2, lambda k: True)
            for i in range(loop_to, last + 1):
                body(i, i % 2, lambda k, i=i: 0 <= i + k < NB)

        def h_bank(k):
            return (bankH[:, 0, :], bankH[:, 1, :], bankM[:, 0, :], bankH[:, 0, :])[k]

        def i_is(i, n):
            return type(i) is int and i == n

        def tile(t, n=1):
            return x[:, bass.ds(t, n), :]

        FFN1 = dict(first=-3, loop_from=3, loop_to=NB - 3, last=NB + 2)
        FFN2 = dict(first=-4, loop_from=2, loop_to=NB - 4, last=NB - 1)

        def split3(eng, out_ap, ah, al, bh, bl):
            eng.matmul(out_ap, ah, bh, start=True, stop=False)
            eng.matmul(out_ap, ah, bl, start=False, stop=False)
            return eng.matmul(out_ap, al, bh, start=False, stop=True)

        def toep_slot(s):
            return toep_early[:, s, :, :, :] if s < EARLY else toep_late[:, s - EARLY, :, :, :]

        def toeplitz(s, c, part, lag):
            return toep_slot(s)[:, c, part, lag:lag + P]

        def u_part(part, b):
            v = u[:, :, part, :].rearrange("p c (h b) -> p h c b", h=2)
            return v[:, :, :, bass.ds(b, 1)].rearrange("p h c o -> p h (c o)")

        u32 = u[:, :, :, :].rearrange("p c s n -> p (c s n)").bitcast(F32).rearrange("p (c n) -> p c n", n=2 * NB)

        def y_of(c, n):
            return u32[:, bass.ds(c, n), :]

        def conv_bank(g):
            b = (bankH, bankM, bankL, bankT)[g % BANKS // 2]
            return b[:, g % 2, :].rearrange("p (c n) -> p c n", n=2 * NB)

        def conv_chunks(chunk):
            for g in range(NCH):
                chunk(g, g % RING)

        @block.sync
        def _(sp):
            sp.dma_start(raw_se[:, :, :], slot_embeds.rearrange("e t d -> (e t) d")
                         .rearrange("(s p) d -> p s d", p=P)).then_inc(w_se, 16)
            for c in range(XCH):
                sp.dma_start(x[:, c * XB * TT:(c + 1) * XB * TT, :],
                             x_dram[:, c * XB * TT:(c + 1) * XB * TT, :]).then_inc(x_in_s[c], 16)
                if c == 0:
                    sp.dma_start(raw_w1[:, :], w1).then_inc(w_w1, 16)
                    for dst, src in ((Alog, A_log), (Bp, B_param), (Cp, C_param)):
                        sp.dma_start(dst[:, :], src).then_inc(w_ssm, 16)
                    sp.dma_start(ldt[:, :], log_dt.rearrange("(d o) -> d o", o=1)).then_inc(w_ssm, 16)
                    sp.dma_start(raw_w2[:, :, :], w2.rearrange("(k p) d -> p k d", p=P)).then_inc(w_w2, 16)
                if c == 1:
                    sp.dma_start(raw_in[:, :, :], in_w.rearrange("(r p) d -> p r d", p=P)).then_inc(w_io, 16)
                    for r in range(2):
                        sp.dma_start(inb[:, r:r + 1], in_b[r * P:(r + 1) * P].rearrange("(p o) -> p o", o=1))\
                          .then_inc(w_io, 16)
                    sp.dma_start(grow[:, :], ln_g.partition_broadcast(P)).then_inc(w_io, 16)
                    sp.dma_start(brow[:, :], ln_b.partition_broadcast(P)).then_inc(w_io, 16)
                    sp.dma_start(raw_out[:, :], out_w).then_inc(w_io, 16)
                    sp.dma_start(obias[:, :], out_b.partition_broadcast(P)).then_inc(w_io, 16)
            sp.wait_ge(resp_s, 4)
            sp.dma_start(resp_dram[:, :, :], respp[:, :, :]).then_inc(resp_out, 16)
            sp.wait_ge(resp_out, 16)
            sp.wait_ge(mix_set, 1)
            for c in range(NCH):
                s = c % RING
                if EARLY <= c < RING:
                    sp.wait_ge((slots_ps, proc_ps, out_ps)[min(c - EARLY, 2)], NB)
                if c >= RING:
                    sp.wait_ge(conv_ps, c - RING + 1)
                for part in range(2):
                    src = bass.AP(resp_dram, c * CH * 2 * KP + part * KP,
                                  [[1, P], [2 * KP, CH], [1, SEQ]])
                    sp.dma_start(toep_slot(s)[:, :, part, :], src).then_inc(toep_s[s], 16)
            with sp.Fori(0, NB // 2 - 1, 1) as j:
                sp.wait_ge(x_s, j * 2 + (NB + 2))
                sp.dma_start(out_dram[:, bass.ds(j * 4, 4), :], x[:, bass.ds(j * 4, 4), :]).then_inc(stored, 16)
            for b in range(NB - 2, NB):
                sp.wait_ge(x_s, NB + b + 1)
                sp.dma_start(out_dram[:, b * TT:(b + 1) * TT, :], x[:, b * TT:(b + 1) * TT, :]).then_inc(stored, 16)
            sp.wait_ge(stored, 16 * (NB // 2 + 1))

        @block.gpsimd
        def _(pool):
            pool.memset(ident[:, :], 0.0).then_inc(consts, 1)
            pool.memset(identb[:, :], 0.0).then_inc(consts, 1)
            pool.memset(flip[:, :], 0.0).then_inc(consts, 1)
            pool.wait_ge(consts, 3)
            for m in (ident, identb):
                pool.affine_select(out=m[:, :], in_=m[:, :], compare_op=ALU.not_equal, fill=1.0, base=0,
                                   pattern=[[-1, P]], channel_multiplier=1).then_inc(consts, 1)
            pool.affine_select(out=flip[:, :], in_=flip[:, :], compare_op=ALU.not_equal, fill=1.0, base=1 - P,
                               pattern=[[1, P]], channel_multiplier=1).then_inc(consts, 1)
            pool.iota(lags[:, :], pattern=[[1, SEQ]], base=0, channel_multiplier=0,
                      allow_small_or_imprecise_dtypes=True).then_inc(consts, 1)
            pool.memset(mhalf[:, :], -0.5).then_inc(consts, 1)
            pool.memset(half[:, :], 0.5).then_inc(consts, 1)
            pool.memset(mone[:, :], -1.0).then_inc(consts, 1)
            pool.memset(zero[:, :], 0.0).then_inc(consts, 1)
            pool.wait_ge(consts, 11)
            count = [0]

            def link(ins):
                count[0] += 1
                ins.then_inc(pool_seq, 1)
                pool.wait_ge(pool_seq, count[0])

            pool.wait_ge(se_floor, 1)
            pool.tensor_tensor(sef[:, :], ms[:, :], mhalf[:, :], ALU.pow).then_inc(se_scale, 1)

            def decay():
                pool.wait_ge(ssm_exp, 2)
                link(pool.tensor_scalar(dt[:, :], expdt[:, :], DT_MIN, DT_MAX, ALU.max, ALU.min))
                link(pool.tensor_scalar(logA[:, :], expA[:, :], dt[:, 0:1], -1.0, ALU.mult, ALU.mult))
                pool.tensor_scalar(logA[:, :], logA[:, :], LOG_A_MIN, 0.0, ALU.max, ALU.min).then_inc(logA_s, 1)

            def w1_parts():
                pool.wait_ge(w_w1, 32)
                link(pool.tensor_tensor(w1g[:, :], raw_w1[:, :], gxcol[:, :].to_broadcast([P, HID]), ALU.mult))
                pool.wait_ge(w1h_s, 1)
                pool.tensor_tensor(w1l[:, :], w1g[:, :], w1h[:, :].bitcast(F32), ALU.subtract).then_inc(w1_s, 1)

            def gains():
                link(pool.tensor_tensor(cb[:, :], Bp[:, :], Cp[:, :], ALU.mult))
                link(pool.tensor_scalar(cb[:, :], cb[:, :], dt[:, 0:1], None, ALU.mult))
                link(pool.tensor_tensor(cbn[:, :], cb[:, :], cb[:, :], ALU.mult))
                link(pool.tensor_tensor(cbn[:, :], cbn[:, :], half[:, :], ALU.pow))
                n = NS // 2
                while n:
                    link(pool.tensor_tensor(cbn[:, 0:n], cbn[:, 0:n], cbn[:, n:2 * n], ALU.add))
                    n //= 2
                link(pool.tensor_scalar(cbs[:, :], cbn[:, 0:1], 1e-18, 1.01 / HALF, ALU.max, ALU.mult))
                link(pool.tensor_tensor(rcbs[:, :], cbs[:, :], mone[:, :], ALU.pow))
                pool.tensor_scalar(cb[:, :], cb[:, :], rcbs[:, 0:1], None, ALU.mult).then_inc(cbs_s, 1)
                pool.wait_ge(cbs_s, 1)

            def response(q):
                n = NS // 4
                pool.wait_ge(powers_s, (q + 1) * n)
                mine = powers[:, q * n:(q + 1) * n, :]
                link(pool.tensor_tensor(mine, mine, cb[:, q * n:(q + 1) * n].unsqueeze(2).to_broadcast([P, n, SEQ]),
                                        ALU.mult))
                while n > 1:
                    n //= 2
                    link(pool.tensor_tensor(mine[:, 0:n, :], mine[:, 0:n, :], mine[:, n:2 * n, :], ALU.add))
                if q > 0:
                    so_far = powers[:, 0, :] if q == 1 else resp[:, :]
                    link(pool.tensor_tensor(resp[:, :], so_far, mine[:, 0, :], ALU.add))

            def response_parts():
                pool.memset(respp[:, :, 0:LAG0], 0.0).then_inc(resp_s, 1)
                pool.memset(respp[:, :, LAG0 + SEQ:KP], 0.0).then_inc(resp_s, 1)
                pool.tensor_copy(respp[:, 0, LAG0:LAG0 + SEQ], resp[:, :]).then_inc(resp_s, 1)
                pool.wait_ge(resp_s, 3)
                pool.tensor_tensor(respp[:, 1, LAG0:LAG0 + SEQ], resp[:, :], respp[:, 0, LAG0:LAG0 + SEQ],
                                   ALU.subtract).then_inc(resp_s, 1)

            def centred(dst, b, done, value):
                t = b * TT
                pool.tensor_tensor(dst, tile(t, TT), nmean[:, bass.ds(t, TT)].unsqueeze(2).to_broadcast([P, TT, D]),
                                   ALU.add).then_inc(done, 1)
                pool.wait_ge(done, value)

            def ffn_scale(base, i, par, has):
                if has(3):
                    pool.wait_ge(var_s, i + (base + 4))
                    pool.tensor_tensor(scale_x[:, 1 - par, :], floor_var[:, 1 - par, :], mhalf[:, 0:TT], ALU.pow)\
                        .then_inc(scale_s, 1)

            def xn_parts(base, i, par, has):
                if has(2):
                    pool.wait_ge(xn_s, i + (base + 3))
                    if has(0):
                        pool.wait_ge(slots_ps, i + (base + 1))
                    pool.tensor_tensor(xnh[:, par, :, 0:D], xn[:, par, :, :],
                                       zero[:, :].unsqueeze(2).to_broadcast([P, TT, D]), ALU.add).then_inc(xnh_s, 1)
                    pool.wait_ge(xnh_s, i + (base + 3))
                    pool.tensor_tensor(xnl[:, par, :, :], xn[:, par, :, :], xnh[:, par, :, 0:D], ALU.subtract)\
                        .then_inc(xnp_s, 1)

            def body1(i, par, has):
                if has(-2):
                    pool.wait_ge(mscale_s, i - 1)
                    if has(-3):
                        pool.wait_ge(mT_ps, i - 2)
                    centred(xc[:, :, :], i - 2, xc_s, i - 1)
                    pool.tensor_tensor(xm[:, :, :], xc[:, :, :], mix_scale[:, par, :].unsqueeze(2).to_broadcast([P, TT, D]),
                                       ALU.mult).then_inc(xm_s, 1)
                    pool.tensor_tensor(rstd[:, bass.ds((i - 2) * TT, TT)], mix_var[:, 1, par, :], mhalf[:, 0:TT],
                                       ALU.pow).then_inc(rstd_s, 1)
                xn_parts(0, i, par, has)
                if i_is(i, 0):
                    pool.wait_ge(n2_s, 1)
                    pool.tensor_tensor(nrm[:, :], n2[:, :], mhalf[:, 0:1], ALU.pow).then_inc(nrm_s, 1)
                ffn_scale(0, i, par, has)
                if i_is(i, -3):
                    decay()
                if has(-1):
                    pool.wait_ge(mvar_s, 2 * i)
                    pool.tensor_tensor(mix_scale[:, 1 - par, :], mix_var[:, 0, 1 - par, :], mhalf[:, 0:TT],
                                       ALU.pow).then_inc(mscale_s, 1)
                if i_is(i, -2):
                    w1_parts()
                if i_is(i, -1):
                    pool.wait_ge(b2_s, 1)
                    pool.tensor_tensor(rb[:, :], b2[:, :], mhalf[:, 0:1], ALU.pow).then_inc(rb_s, 1)
                    gains()
                if i_is(i, 0):
                    for q in range(3):
                        response(q)
                if i_is(i, 1):
                    response(3)
                if i_is(i, 2):
                    response_parts()

            def residual(i, has):
                c = i + 4
                if has(3):
                    pool.wait_ge(upd_s, c)
                centred(res[:, :, :], c, rc_s, i + 5)
                pool.tensor_tensor(res2[:, :, :], res[:, :, :],
                                   rstd[:, bass.ds(c * TT, TT)].unsqueeze(2).to_broadcast([P, TT, D]),
                                   ALU.mult).then_inc(res_s, 1)
                pool.wait_ge(res_s, i + 5)
                pool.tensor_tensor(resb[:, :, :], res2[:, :, :], obias[:, :].unsqueeze(1).to_broadcast([P, TT, D]),
                                   ALU.add).then_inc(resb_s, 1)

            def body2(i, par, has):
                if i_is(i, -4):
                    residual(i, has)
                    pool.wait_ge(z_s, NB)
                    pool.wait_ge(y_s, NCH + BANKS)
                if has(4):
                    if has(3):
                        pool.wait_ge(ygT_ps, i + 4)
                    y = u32[:, :, :].rearrange("p c (h b) -> p h c b", h=2)[:, :, :, bass.ds(i + 4, 1)]
                    pool.tensor_tensor(yg[:, :, :], y.rearrange("p h c o -> p h (c o)"),
                                       z[:, :, bass.ds(i + 4, 1), :].rearrange("p h o c -> p h (o c)"),
                                       ALU.mult).then_inc(yg_s, 1)
                    if not i_is(i, -4):
                        residual(i, has)
                xn_parts(NB, i, par, has)
                ffn_scale(NB, i, par, has)

            steps(pool, body1, **FFN1)
            pool.wait_ge(mT_ps, NB)
            pool.wait_ge(rstd_s, NB)
            steps(pool, body2, **FFN2)

        @block.scalar
        def _(act):
            act.dma_start(gslot[:, :], gamma_slot.partition_broadcast(P)).then_inc(w_g, 16)
            act.dma_start(gxrow[:, :], gamma_x.partition_broadcast(P)).then_inc(w_g, 16)
            act.dma_start(gxcol[:, :], gamma_x.rearrange("(d o) -> d o", o=1)).then_inc(w_w1, 16)
            act.wait_ge(w_se, 16)
            for s in range(ST):
                e = act.activation(sq[:, s, :], raw_se[:, s, :], ACT.Square, accum_out=ss[:, s:s + 1])
            e.then_inc(se_sum, 1)
            act.wait_ge(w_ssm, 64)
            act.activation(expA[:, :], Alog[:, :], ACT.Exp).then_inc(ssm_exp, 1)
            act.activation(expdt[:, :], ldt[:, :], ACT.Exp).then_inc(ssm_exp, 1)
            act.wait_ge(w_w1, 32)
            act.activation(w1h[:, :], raw_w1[:, :], ACT.Copy, scale=gxcol[:, 0:1]).then_inc(w1h_s, 1)
            act.activation(w1sq[:, :], raw_w1[:, :], ACT.Square, scale=gxcol[:, 0:1], accum_out=w1sum[:, :])\
               .then_inc(wsum_s, 1)
            act.wait_ge(w_w2, 16)
            act.activation(w2sq[:, :, :], raw_w2[:, :, :], ACT.Square).then_inc(wsum_s, 1)
            act.wait_ge(logA_s, 1)
            act.wait_ge(consts, 7)
            for n in range(NS):
                act.activation(powers[:, n, :], lags[:, :], ACT.Exp, scale=logA[:, n:n + 1]).then_inc(powers_s, 1)

            def second_half(base, i):
                act.wait_ge(sT_ps, i + (base + 1))
                act.activation(sTh[:, :], bankM[:, 0, :], ACT.Copy).then_inc(sTh_s, 1)
                for k in range(HT):
                    act.wait_ge(h_ps[k], i + (base + 1))
                    act.activation(hT[:, k, :], h_bank(k), ACT.Gelu).then_inc(gelu_s[k], 1)

            def combine_weights(base, i, nxt):
                act.wait_ge(nrmax_s, i + (base + 2))
                for t in range(TT):
                    act.activation(E_c[:, t, :], bankL[:, t, :], ACT.Exp, bias=nrowmax[:, t:t + 1],
                                   accum_out=rowsum[:, nxt, t:t + 1]).then_inc(Ec_s[t], 1)

            def parts(base, i, nxt, has):
                if has(1):
                    for t in range(TT):
                        act.wait_ge(Ld_ps[t], i + (base + 2))
                        e = act.activation(E_dh[:, t, :], bankL[:, t, :], ACT.Exp)
                    e.then_inc(Edh_s, 1)
                if has(0):
                    act.wait_ge(proc_ps, i + (base + 1))
                    act.activation(proch[:, :, :].rearrange("p s d -> p (s d)"), bankH[:, 1, :], ACT.Copy)\
                       .then_inc(proch_s, 1)
                if has(1):
                    for t in range(TT):
                        act.activation(E_d[:, t, :], bankL[:, t, :], ACT.Exp).then_inc(Ed_s[t], 1)

            def transposed_weights(base, i, nxt):
                act.wait_ge(EcT_ps, i + (base + 2))
                act.activation(E_cTh[:, nxt, :, :], LT, ACT.Copy, scale=HALF).then_inc(EcTh_s, 1)
                act.wait_ge(rslot_s, i + (base + 2))
                for s in range(2):
                    e = act.activation(slots_n[:, 2 + s, :], slot_ps[:, 1, s, 0:D], ACT.Copy, scale=rslot[:, 1, s:s + 1])
                e.then_inc(slots_s[1], 1)

            def body1(i, par, has):
                if has(0):
                    second_half(0, i)
                if has(1):
                    combine_weights(0, i, 1 - par)
                if has(-2):
                    act.wait_ge(mT_ps, i - 1)
                    act.activation(mT[:, :], bankH[:, 0, :], ACT.Copy).then_inc(mT_s, 1)
                parts(0, i, 1 - par, has)
                if has(-2):
                    uz = bankM[:, 0, :].rearrange("p (h r c) -> p h r c", h=2, r=2)
                    act.wait_ge(uz_ps, i - 1)
                    act.activation(u_part(0, i - 2), uz[:, :, 0, :], ACT.Copy).then_inc(uh_s, 1)
                    if has(-3):
                        act.wait_ge(e1_s, i - 2)
                    act.activation(sig[:, :, :], uz[:, :, 1, :], ACT.Exp, scale=-1.0).then_inc(e_s, 1)
                    act.activation(z[:, :, bass.ds(i - 2, 1), :].rearrange("p h o c -> p h (o c)"), uz[:, :, 1, :],
                                   ACT.Copy).then_inc(zc_s, 1)
                if has(1):
                    transposed_weights(0, i, 1 - par)

            def body2(i, par, has):
                if has(0):
                    second_half(NB, i)
                if has(1):
                    combine_weights(NB, i, 1 - par)
                if has(4):
                    act.wait_ge(ygT_ps, i + 5)
                    act.activation(mT[:, 0:SEQ], bankH[:, 0, 0:SEQ], ACT.Copy).then_inc(ygT_s, 1)
                parts(NB, i, 1 - par, has)
                if has(1):
                    transposed_weights(NB, i, 1 - par)

            steps(act, body1, **FFN1)

            act.sem_inc(y_s, BANKS)

            def take_y(g, s):
                act.wait_ge(conv_ps, g + 1)
                act.activation(y_of(g * CH, CH), conv_bank(g), ACT.Copy).then_inc(y_s, 1)
            conv_chunks(take_y)
            steps(act, body2, **FFN2)

        @block.vector
        def _(dve):
            count = [0]

            def link(ins):
                count[0] += 1
                ins.then_inc(dve_seq, 1)
                dve.wait_ge(dve_seq, count[0])

            for h in range(2):
                dve.memset(xnh[:, h, :, D:D + 1], 1.0)
            dve.memset(ones[:, :], 1.0).then_inc(ones_s, 1)
            link(dve.memset(brep[:, 0:P], 0.0))
            link(dve.memset(brep[0:1, 0:P], 1.0))
            link(dve.memset(brep[64:65, 0:P], 1.0))
            dve.tensor_copy(oneh[:, :], brep[:, 0:P]).then_inc(ones_s, 1)
            dve.wait_ge(w_g, 32)
            dve.wait_ge(w_se, 16)
            link(dve.tensor_tensor(gslot[:, :], gslot[:, :], gxrow[:, :], ALU.mult))
            dve.tensor_tensor(se_n[:, :, :], raw_se[:, :, :],
                              gslot[:, :].unsqueeze(1).to_broadcast([P, ST, D]), ALU.mult).then_inc(se_row, 1)
            dve.wait_ge(se_sum, 1)
            dve.tensor_scalar(ms[:, :], ss[:, :], 1.0 / D, RMS_EPS * RMS_EPS / D, ALU.mult, ALU.max).then_inc(se_floor, 1)

            def slots_scale():
                dve.wait_ge(se_row, 1)
                dve.wait_ge(se_scale, 1)
                for s in range(ST):
                    e = dve.tensor_scalar(se_n[:, s, :], se_n[:, s, :], sef[:, s:s + 1], None, ALU.mult)
                e.then_inc(se_row, 1)

            def slots_parts():
                dve.wait_ge(seT_ps, 1)
                link(dve.tensor_copy(seh[:, :], bankH[:, 0, :]))
                dve.tensor_tensor(sel[:, :], bankH[:, 0, :], seh[:, :].bitcast(F32), ALU.subtract).then_inc(se_s, 1)

            def in_rows():
                dve.wait_ge(w_io, 112)
                link(dve.tensor_tensor(inw[:, :, :], raw_in[:, :, :],
                                       brow[:, :].unsqueeze(1).to_broadcast([P, 2, D]), ALU.mult))
                link(dve.reduce_sum(bias[:, :], inw[:, :, :], AX))
                link(dve.tensor_tensor(bias[:, :], bias[:, :], inb[:, :], ALU.add))
                link(dve.tensor_tensor(inw[:, :, :], raw_in[:, :, :],
                                       grow[:, :].unsqueeze(1).to_broadcast([P, 2, D]), ALU.mult))
                link(dve.tensor_tensor(insq[:, 0, :], inw[:, 0, :], inw[:, 0, :], ALU.mult))
                link(dve.reduce_sum(n2[:, :], insq[:, 0, :], AX))
                dve.tensor_scalar(n2[:, :], n2[:, :], float(D) * 1.01, 1e-30, ALU.mult, ALU.max).then_inc(n2_s, 1)

            def in_scale():
                dve.wait_ge(n2_s, 1)
                dve.wait_ge(nrm_s, 1)
                link(dve.tensor_scalar(nbias[:, :], bias[:, 0:1], -1.0, None, ALU.mult))
                link(dve.tensor_tensor(nbias[:, :], bias[:, 0:1], nbias[:, :], ALU.max))
                link(dve.scalar_tensor_tensor(out=ubound[:, :], in0=n2[:, :], scalar=nrm[:, 0:1], in1=nbias[:, :],
                                              op0=ALU.mult, op1=ALU.add))
                link(dve.tensor_scalar(ubound[:, :], ubound[:, :], 1.0 / HALF, None, ALU.mult))
                link(dve.reciprocal(rub[:, :], ubound[:, :]))
                link(dve.tensor_scalar(inw[:, 0, :], inw[:, 0, :], rub[:, 0:1], None, ALU.mult))
                link(dve.tensor_scalar(bias[:, 0:1], bias[:, 0:1], rub[:, 0:1], None, ALU.mult))
                dve.wait_ge(cbs_s, 1)
                dve.tensor_scalar(oscale[:, :], ubound[:, :], cbs[:, 0:1], None, ALU.mult).then_inc(in_row, 1)

            def in_parts():
                dve.wait_ge(inT_ps, 1)
                dve.tensor_copy(brep[:, :], bankH[:, 0, 0:2 * D]).then_inc(bias_s, 1)
                dve.tensor_copy(inT[:, :], bankM[:, 0, 0:2 * D])
                dve.tensor_scalar(outT[:, :], bankM[:, 0, 2 * D:3 * D], oscale[:, 0:1], None, ALU.mult)\
                   .then_inc(inT_s, 1)

            def bias_parts():
                dve.wait_ge(bias_s, 1)
                link(dve.tensor_copy(binh[:, :], brep[:, :]))
                link(dve.tensor_tensor(brep[:, :], brep[:, :], binh[:, :].bitcast(F32), ALU.subtract))
                dve.tensor_copy(binh[64:P, :], brep[64:P, :]).then_inc(mix_set, 1)

            def proc_bound():
                dve.wait_ge(bound_ps, 1)
                link(dve.reduce_max(w2max[:, :], bankH[:, 1, 0:D], AX))
                link(dve.tensor_tensor(b2[:, :], w2max[:, :], bankH[:, 1, D:D + 1], ALU.mult))
                dve.tensor_scalar(b2[:, :], b2[:, :], D * 1.01 / (WIDE * WIDE), 1e-30, ALU.mult, ALU.max)\
                   .then_inc(b2_s, 1)

            def w2_scale():
                dve.wait_ge(rb_s, 1)
                dve.wait_ge(w_w2, 16)
                dve.tensor_scalar(w2s[:, :, :], raw_w2[:, :, :], rb[:, 0:1], None, ALU.mult).then_inc(w2_s, 1)
                link(dve.reciprocal(bscale[:, :], rb[:, :]))
                link(dve.tensor_scalar(cscale[:, :], bscale[:, :], 0.5 / HALF, None, ALU.mult))

            def silu_z(i):
                z_b = z[:, :, bass.ds(i - 3, 1), :].rearrange("p h o c -> p h (o c)")
                dve.wait_ge(e_s, i - 2)
                dve.tensor_scalar(upd[:, :, :], sig[:, :, :], 1.0, None, ALU.add).then_inc(e1_s, 1)
                dve.wait_ge(e1_s, i - 2)
                dve.reciprocal(rsig[:, :, :], upd[:, :, :]).then_inc(sig_s, 1)
                dve.wait_ge(sig_s, i - 2)
                dve.wait_ge(zc_s, i - 2)
                dve.tensor_tensor(z_b, z_b, rsig[:, :, :], ALU.mult).then_inc(z_s, 1)

            def negate_rowmax(base, i):
                dve.wait_ge(rmax_s, i + (base + 2))
                dve.tensor_scalar(nrowmax[:, :], rowmax[:, :], -1.0, None, ALU.mult).then_inc(nrmax_s, 1)

            def ffn_body(base, i, par, has):
                first = base == 0
                nxt = 1 - par
                if has(1):
                    if first and has(-1):
                        dve.wait_ge(x_s, i)
                    if not first and has(3):
                        dve.wait_ge(mixed, i + 4)
                    dve.wait_ge(L_ps, i + (base + 2))
                    dve.reduce_max(rowmax[:, :], bankL[:, :, :], AX).then_inc(rmax_s, 1)
                    ahead = i_is(i, -1)
                    if ahead:
                        negate_rowmax(base, i)
                    dve.wait_ge(LT_ps, i + (base + 2))
                    dve.reduce_max(colmax[:, :], LT, AX).then_inc(cmax_s, 1)
                    if not ahead:
                        negate_rowmax(base, i)
                    dve.wait_ge(cmax_s, i + (base + 2))
                    for k, slack in enumerate((ROUND, -ROUND)):
                        e = dve.tensor_scalar(ncm[:, k, :], colmax[:, :], -1.0 - slack, SHIFT, ALU.mult, ALU.add)
                    e.then_inc(ncm_s, 1)
                    dve.wait_ge(ncm_s, i + (base + 2))
                    dve.tensor_tensor(ncolmax[:, :], ncm[:, 0, :], ncm[:, 1, :], ALU.min).then_inc(ncmax_s, 1)
                elif first and has(-1):
                    dve.wait_ge(x_s, i)
                elif not first and has(3):
                    dve.wait_ge(mixed, i + 4)
                if first and i_is(i, 1):
                    in_scale()
                if has(2):
                    dve.wait_ge(xT_ps, i + (base + 3))
                    dve.tensor_copy(xTh[:, par, :], bankM[:, 1, 0:SEQ]).then_inc(xTh_s, 1)
                    dve.wait_ge(xTh_s, i + (base + 3))
                    dve.tensor_tensor(xTl[:, par, :], bankM[:, 1, 0:SEQ], xTh[:, par, :].bitcast(F32),
                                      ALU.subtract).then_inc(xT_s, 1)
                if first and i_is(i, -2):
                    slots_parts()
                if first and i_is(i, -1):
                    proc_bound()
                if has(3):
                    if first and type(i) is int and (i + 3) % XB == 0:
                        dve.wait_ge(x_in_s[(i + 3) // XB], 16)
                    if first and i_is(i, 2):
                        for c in range((i + 3) // XB + 1, XCH):
                            dve.wait_ge(x_in_s[c], 16)
                    for t in range(TT):
                        e = dve.bn_stats(bn6[:, t, :], tile((i + 3) * TT + t).rearrange("p o d -> p (o d)"))
                    e.then_inc(bn_s, 1)
                again = first and has(-1)
                if again:
                    for t in range(TT):
                        e = dve.bn_stats(bnm[:, t, :], tile((i - 1) * TT + t).rearrange("p o d -> p (o d)"))
                    e.then_inc(mbn_s, 1)
                if first and i_is(i, 0):
                    in_rows()
                if first and i_is(i, 2):
                    bias_parts()
                draining = type(i) is int and i >= NB
                if first and has(-3) and not draining:
                    silu_z(i)
                if has(3):
                    dve.wait_ge(bn_s, i + (base + 4))
                if again:
                    dve.wait_ge(mbn_s, i)
                if has(0):
                    dve.wait_ge(proch_s, i + (base + 1))
                    dve.tensor_tensor(procl[:, :, :].rearrange("p s d -> p (s d)"), bankH[:, 1, :],
                                      proch[:, :, :].rearrange("p s d -> p (s d)"), ALU.subtract).then_inc(proc_s, 1)
                if has(1):
                    for t in range(TT):
                        dve.wait_ge(Ed_s[t], i + (base + 2))
                        e = dve.tensor_tensor(E_dl[:, t, :], E_d[:, t, :], E_dh[:, t, :], ALU.subtract)
                    e.then_inc(Edl_s, 1)
                if has(3):
                    for t in range(TT):
                        e = dve.bn_aggr(mean_var[:, nxt, t, :], bn6[:, t, :])
                    e.then_inc(mv_s, 1)
                if again:
                    for t in range(TT):
                        e = dve.bn_aggr(new_mv[:, t, :], bnm[:, t, :])
                    e.then_inc(mag_s, 1)
                if has(3):
                    dve.wait_ge(mv_s, i + (base + 4))
                    dve.tensor_scalar(floor_var[:, nxt, :], mean_var[:, nxt, :, 1],
                                      LN_EPS * RMS_EPS * RMS_EPS / D, None, ALU.max).then_inc(var_s, 1)
                if again:
                    dve.wait_ge(mag_s, i)
                    if has(-3) and not has(3):
                        dve.wait_ge(rstd_s, i - 2)
                    dve.tensor_scalar(mix_var[:, 0, nxt, :], new_mv[:, :, 1], 1.0 + LN_EPS, LN_EPS * LN_EPS,
                                      ALU.mult, ALU.add)
                    dve.tensor_scalar(mix_var[:, 1, nxt, :], new_mv[:, :, 1], LN_EPS, None, ALU.add).then_inc(mvar_s, 1)
                    dve.tensor_scalar(nmean[:, bass.ds((i - 1) * TT, TT)], new_mv[:, :, 0], -1.0, None, ALU.mult)\
                       .then_inc(mvar_s, 1)
                if first and i_is(i, 1):
                    in_parts()
                if first and has(-3) and draining:
                    silu_z(i)
                side = not first and has(4)
                if first and has(-2):
                    uz = bankM[:, 0, :].rearrange("p (h r c) -> p h r c", h=2, r=2)
                    dve.wait_ge(uh_s, i - 1)
                    dve.wait_ge(zc_s, i - 1)
                    dve.tensor_tensor(u_part(1, i - 2), uz[:, :, 0, :], u_part(0, i - 2), ALU.subtract).then_inc(u_s, 1)
                if side:
                    dve.wait_ge(resb_s, i + 5)
                    dve.wait_ge(o_ps, i + 5)
                    dve.tensor_tensor(upd[:, :, :], bankM[:, 0, 0:SEQ].rearrange("p (h d) -> p h d", h=2),
                                      resb[:, :, :], ALU.add).then_inc(upd_s, 1)
                if has(1):
                    dve.wait_ge(slots_ps, i + (base + 2))
                    dve.reciprocal(rslot[:, :, :], slot_ps[:, :, :, D]).then_inc(rslot_s, 1)
                    dve.wait_ge(Ec_s[TT - 1], i + (base + 2))
                    dve.reciprocal(rrow[:, :], rowsum[:, nxt, :]).then_inc(rrow_s, 1)
                    dve.wait_ge(rslot_s, i + (base + 2))
                    dve.tensor_tensor(slots_n[:, 0:2, :], slot_ps[:, 0, :, 0:D],
                                      rslot[:, 0, :].unsqueeze(2).to_broadcast([P, 2, D]), ALU.mult)\
                       .then_inc(slots_s[0], 1)
                if has(1):
                    dve.wait_ge(EcTh_s, i + (base + 2))
                    dve.scalar_tensor_tensor(out=E_cTl[:, nxt, :, :], in0=LT, scalar=HALF, in1=E_cTh[:, nxt, :, :],
                                             op0=ALU.mult, op1=ALU.subtract).then_inc(EcT_s, 1)
                    dve.wait_ge(sTh_s, i + (base + 2))
                    dve.tensor_tensor(sTl[:, :], bankM[:, 0, :], sTh[:, :].bitcast(F32), ALU.subtract).then_inc(sT_s, 1)
                if side:
                    dve.wait_ge(upd_s, i + 5)
                    dve.tensor_scalar(updc[:, :, :], upd[:, :, :], CLIP, -CLIP, ALU.min, ALU.max).then_inc(updc_s, 1)
                if first and i_is(i, -1):
                    w2_scale()
                if has(1):
                    dve.wait_ge(rrow_s, i + (base + 2))
                    dve.tensor_scalar(hrrow[:, nxt, :], rrow[:, :], cscale[:, 0:1], None, ALU.mult).then_inc(hrrow_s, 1)
                if side:
                    dve.wait_ge(updc_s, i + 5)
                    dve.tensor_tensor(tile((i + 4) * TT, TT), tile((i + 4) * TT, TT), updc[:, :, :], ALU.add)\
                       .then_inc(mixed, 1)
                if first and i_is(i, -3):
                    slots_scale()
                if has(3):
                    dve.wait_ge(scale_s, i + (base + 4))
                    for t in range(TT):
                        e = dve.tensor_scalar(xn[:, nxt, t, 0:D].unsqueeze(1), tile((i + 3) * TT + t),
                                              mean_var[:, nxt, t, 0:1], scale_x[:, nxt, t:t + 1],
                                              ALU.subtract, ALU.mult)
                    e.then_inc(xn_s, 1)
                if has(0):
                    dve.wait_ge(hrrow_s, i + (base + 1))
                    dve.wait_ge(out_ps, i + (base + 1))
                    for t in range(TT):
                        n = i * TT + t
                        e = dve.scalar_tensor_tensor(out=tile(n), in0=bankM[:, 1, t * D:(t + 1) * D].unsqueeze(1),
                                                     scalar=hrrow[:, par, t:t + 1], in1=tile(n),
                                                     op0=ALU.mult, op1=ALU.add)
                    e.then_inc(x_s, 1)
            steps(dve, lambda i, par, has: ffn_body(0, i, par, has), **FFN1)
            steps(dve, lambda i, par, has: ffn_body(NB, i, par, has), **FFN2)

        @block.tensor
        def _(pe):
            def combine_hi(par, t):
                for s in range(ST):
                    for n, m in enumerate((E_cTh, E_cTl)):
                        pe.matmul(bankM[:, 1, t * D:(t + 1) * D], m[:, par, s, t * P:(t + 1) * P], proch[:, s, :],
                                  start=(s == 0 and n == 0), stop=False)

            def combine_lo(par, t):
                for s in range(ST):
                    e = pe.matmul(bankM[:, 1, t * D:(t + 1) * D], E_cTh[:, par, s, t * P:(t + 1) * P],
                                  procl[:, s, :], start=False, stop=(s == ST - 1))
                return e

            def set_up_slots():
                pe.wait_ge(se_row, 2)
                for s in range(ST):
                    e = pe.transpose(bankH[:, 0, s * P:(s + 1) * P], se_n[:, s, :], ident[:, :])
                e.then_inc(seT_ps, 1)
                pe.wait_ge(ones_s, 1)
                pe.wait_ge(wsum_s, 2)
                for k in range(HT):
                    pe.matmul(bankH[:, 1, 0:D], ones[:, :], w2sq[:, k, :], start=(k == 0), stop=(k == HT - 1))
                pe.matmul(bankH[:, 1, D:D + 1], ones[:, :], w1sum[:, :], start=True, stop=True).then_inc(bound_ps, 1)

            def set_up_mixer():
                pe.wait_ge(in_row, 1)
                pe.wait_ge(w_io, 112)
                for r in range(2):
                    pe.transpose(bankM[:, 0, r * D:(r + 1) * D], inw[:, r, :], ident[:, :])
                    pe.matmul(bankH[:, 0, r * D:(r + 1) * D], bias[:, r:r + 1].to_broadcast([P, P]), ident[:, :],
                              start=True, stop=True)
                pe.transpose(bankM[:, 0, 2 * D:3 * D], raw_out[:, :], ident[:, :]).then_inc(inT_ps, 1)

            def logits_begin(base, i, nxt):
                pe.wait_ge(xT_s, i + (base + 2))
                if base == 0 and i_is(i, -1):
                    pe.wait_ge(se_s, 1)
                pe.matmul(bankL[:, 0, :], xTh[:, nxt, 0:P], seh[:, :], start=True, stop=False)

            def logits_end(base, i, par, has):
                nxt = 1 - par
                pe.matmul(bankL[:, 0, :], xTh[:, nxt, 0:P], sel[:, :], start=False, stop=False)
                pe.matmul(bankL[:, 0, :], xTl[:, nxt, 0:P], seh[:, :], start=False, stop=True)
                split3(pe, bankL[:, 1, :], xTh[:, nxt, P:SEQ], xTl[:, nxt, P:SEQ], seh[:, :], sel[:, :])\
                    .then_inc(L_ps, 1)
                if has(0):
                    pe.wait_ge(EcT_s, i + (base + 1))
                for s in range(ST):
                    e = pe.matmul(LT[:, s, :], seh[:, s * P:(s + 1) * P], xTh[:, nxt, :], start=True, stop=True)
                e.then_inc(LT_ps, 1)

            def ffn_body(base, i, par, has):
                first = base == 0
                nxt = 1 - par
                side = has(-2) if first else has(4)
                n_side = i - 1 if first else i + 5
                if has(1):
                    logits_begin(base, i, nxt)
                if has(0):
                    if first and i_is(i, 2):
                        pe.wait_ge(inT_s, 1)
                    if first and has(-3):
                        pe.wait_ge(u_s, i - 2)
                    if not first:
                        pe.wait_ge(upd_s, min(i + 4, NB) if type(i) is int else i + 4)
                    for s in range(ST):
                        if s % 2 == 0:
                            pe.wait_ge(slots_s[s // 2], i + (base + 1))
                        e = pe.transpose(bankM[:, 0, s * P:(s + 1) * P], slots_n[:, s, :], ident[:, :])
                    e.then_inc(sT_ps, 1)
                if has(1):
                    logits_end(base, i, par, has)
                if has(0):
                    pe.wait_ge(sT_s, i + (base + 1))
                    if first and i_is(i, 0):
                        pe.wait_ge(w1_s, 1)
                        pe.wait_ge(w2_s, 1)
                    for k in range(HT):
                        if k == 3:
                            pe.wait_ge(gelu_s[0], i + (base + 1))
                        split3(pe, h_bank(k), w1h[:, k * P:(k + 1) * P], w1l[:, k * P:(k + 1) * P],
                               sTh[:, :], sTl[:, :]).then_inc(h_ps[k], 1)
                if has(2):
                    pe.wait_ge(xn_s, i + (base + 3))
                    if has(-1):
                        pe.wait_ge(x_s, i + base)
                    if has(1):
                        pe.wait_ge(xT_s, i + (base + 2))
                    for t in range(TT):
                        e = pe.transpose(bankM[:, 1, t * P:(t + 1) * P], xn[:, par, t, :], ident[:, :])
                    e.then_inc(xT_ps, 1)
                if first and i_is(i, -2):
                    set_up_slots()
                if has(0):
                    for k in range(2):
                        pe.wait_ge(gelu_s[1 + k], i + (base + 1))
                        project(k)
                if side:
                    if has(0):
                        pe.wait_ge(gelu_s[3], i + (base + 1))
                    if first:
                        pe.wait_ge(xm_s, n_side)
                        for t in range(TT):
                            pe.transpose(bankH[:, 0, t * P:(t + 1) * P], xm[:, t, :], ident[:, :])
                            e = pe.transpose(bankH[:, 0, SEQ + t * P:SEQ + (t + 1) * P], xm[:, t, :], flip[:, :])
                        e.then_inc(mT_ps, 1)
                    else:
                        pe.wait_ge(yg_s, n_side)
                        for t in range(TT):
                            e = pe.transpose(bankH[:, 0, t * P:(t + 1) * P], yg[:, t, :], ident[:, :])
                        e.then_inc(ygT_ps, 1)

                def less_colmax(t):
                    pe.wait_ge(Ec_s[t], i + (base + 2))
                    pe.wait_ge(ncmax_s, i + (base + 2))
                    for s in range(ST):
                        e = pe.matmul(bankL[:, t, s * P:(s + 1) * P], ncolmax[:, s:s + 1].to_broadcast([P, P]),
                                      identb[:, :], start=False, stop=True, skip_group_check=True)
                    e.then_inc(Ld_ps[t], 1)

                if has(0):
                    pe.wait_ge(gelu_s[3], i + (base + 1))
                    project(2)
                for t in range(TT):
                    if has(1):
                        less_colmax(t)
                    if has(0):
                        e = project(3, range(t, 1 + t * (ST - 1)))
                if has(0):
                    e.then_inc(proc_ps, 1)
                if has(1):
                    if first and i_is(i, 1):
                        set_up_mixer()
                    for s in range(ST):
                        for t in range(TT):
                            e = pe.transpose(LT[:, s, t * P:(t + 1) * P], E_c[:, t, s * P:(s + 1) * P], ident[:, :])
                    e.then_inc(EcT_ps, 1)
                if side and first:
                    pe.wait_ge(mT_s, n_side)
                    if i_is(i, 2):
                        pe.wait_ge(mix_set, 1)
                        pe.wait_ge(ones_s, 2)
                    if not has(0):
                        pe.wait_ge(u_s, i - 2)
                    for t in range(TT):
                        dst = bankM[:, 0, t * 2 * D:(t + 1) * 2 * D]
                        pe.matmul(dst, oneh[:, :], binh[:, :], start=True, stop=False, skip_group_check=True)
                        pe.matmul(dst[:, 0:D], mT[:, SEQ + t * P:SEQ + (t + 1) * P], inT[:, 0:D],
                                  start=False, stop=True, skip_group_check=True)
                        e = pe.matmul(dst[:, D:2 * D], mT[:, t * P:(t + 1) * P], inT[:, D:2 * D],
                                      start=False, stop=True, skip_group_check=True)
                    e.then_inc(uz_ps, 1)
                if side and not first:
                    pe.wait_ge(ygT_s, n_side)
                    if not has(0) and has(3):
                        pe.wait_ge(upd_s, i + 4)
                    for t in range(TT):
                        e = pe.matmul(bankM[:, 0, t * D:(t + 1) * D], mT[:, t * P:(t + 1) * P], outT[:, :],
                                      start=True, stop=True)
                    e.then_inc(o_ps, 1)

                def slots_passes(parts, tiles, first_pass, last_pass):
                    for s in tiles:
                        dst = slot_ps[:, s // 2, s % 2, :]
                        for n, (ed, xp, cols) in enumerate(parts):
                            for t in range(TT):
                                e = pe.matmul(dst[:, 0:cols], ed[:, t, s * P:(s + 1) * P], xp[:, nxt, t, :],
                                              start=(first_pass and s % 2 == 0 and n == 0 and t == 0),
                                              stop=(last_pass and t == TT - 1), skip_group_check=True)
                    return e

                if has(1):
                    pe.wait_ge(Edh_s, i + (base + 2))
                    pe.wait_ge(xnp_s, i + (base + 2))
                    if first and i_is(i, -1):
                        pe.wait_ge(b2_s, 1)
                    if first and i_is(i, 1):
                        pe.wait_ge(bias_s, 1)
                    if side:
                        pe.wait_ge(mT_s if first else ygT_s, n_side)
                    hi = ((E_dh, xnh, D + 1), (E_dh, xnl, D))
                    slots_passes(hi, (0, 1), True, False)
                    if has(0):
                        pe.wait_ge(proc_s, i + (base + 1))
                    slots_passes(hi, (2, 3), True, False)
                if has(0):
                    if has(2):
                        pe.wait_ge(xT_s, i + (base + 3))
                    else:
                        pe.wait_ge(x_s, i + base)
                    pe.wait_ge(proch_s, i + (base + 1))
                    combine_hi(par, 0)
                    pe.wait_ge(proc_s, i + (base + 1))
                    combine_lo(par, 0)
                if has(1):
                    pe.wait_ge(Edl_s, i + (base + 2))
                    slots_passes(((E_dl, xnh, D + 1),), range(ST), False, True).then_inc(slots_ps, 1)
                if has(0):
                    combine_hi(par, 1)
                    combine_lo(par, 1).then_inc(out_ps, 1)

            def project(k, tiles=range(ST)):
                for s in tiles:
                    e = pe.matmul(bankH[:, 1, s * D:(s + 1) * D], hT[:, k, s * P:(s + 1) * P], w2s[:, k, :],
                                  start=(k == 0 and s == 0), stop=(k == HT - 1), skip_group_check=True)
                return e

            pe.wait_ge(consts, 11)
            steps(pe, lambda i, par, has: ffn_body(0, i, par, has), **FFN1)

            pe.wait_ge(u_s, NB)
            pe.wait_ge(x_s, NB)

            def convolve(g, s):
                pe.wait_ge(toep_s[s], g // RING * 32 + 32)
                pe.wait_ge(y_s, g + 1)
                for c in range(CH):
                    dst = conv_bank(g)[:, c, :]
                    uc = u[:, bass.ds(g * CH + c, 1), :, :]
                    uh = uc[:, :, 0, :].rearrange("p o n -> p (o n)")
                    ul = uc[:, :, 1, :].rearrange("p o n -> p (o n)")
                    near = [toeplitz(s, c, part, 0) for part in range(2)]
                    far = [toeplitz(s, c, part, P) for part in range(2)]
                    pe.matmul(dst, near[0], uh, start=True, stop=False, skip_group_check=True)
                    pe.matmul(dst, near[0], ul, start=False, stop=False, skip_group_check=True)
                    pe.matmul(dst, near[1], uh, start=False, stop=False, skip_group_check=True)
                    pe.matmul(dst[:, NB:], far[0], uh[:, 0:NB], start=False, stop=False, skip_group_check=True)
                    pe.matmul(dst[:, NB:], far[0], ul[:, 0:NB], start=False, stop=False, skip_group_check=True)
                    e = pe.matmul(dst[:, NB:], far[1], uh[:, 0:NB], start=False, stop=True, skip_group_check=True)
                e.then_inc(conv_ps, 1)
            conv_chunks(convolve)
            steps(pe, lambda i, par, has: ffn_body(NB, i, par, has), **FFN2)


_INS = ['L0_attn_x', 'L0_attn_A_log', 'L0_attn_B_param', 'L0_attn_C_param', 'L0_attn_log_dt', 'L0_attn_in_w',
        'L0_attn_in_b', 'L0_attn_out_w', 'L0_attn_out_b', 'L0_attn_ln_g', 'L0_attn_ln_b', 'L0_ffn_gamma_x',
        'L0_ffn_gamma_slot', 'L0_ffn_slot_embeds', 'L0_ffn_w1', 'L0_ffn_w2']


def kernel(**inputs):
    import numpy as _np
    import concourse.bacc as _bacc
    from concourse import mybir as _mybir
    from concourse.bass_utils import run_bass_kernel_spmd as _run

    nc = _bacc.Bacc("TRN2", target_bir_lowering=False, num_devices=1)
    arrays, args = {}, []
    for name in _INS:
        a = _np.ascontiguousarray(inputs[name])
        arrays[f"in_{name}"] = a
        args.append(nc.dram_tensor(f"in_{name}", a.shape, _mybir.dt.from_np(a.dtype), kind="ExternalInput").ap())
    args.append(nc.dram_tensor("out_x", inputs['L0_attn_x'].shape, _mybir.dt.from_np(_np.dtype("float32")),
                               kind="ExternalOutput").ap())
    macaron_kernel(nc, *args)
    return _run(nc, [arrays], core_ids=[0]).results[0]["out_x"]
```
